# Optimizing a Trainium2 kernel written in Bass

```python
import numpy as np
import jax
import jax.numpy as jnp

def _softmax(x, axis=-1):
    return jax.nn.softmax(x, axis=axis)

def _gelu(x):
    return jax.nn.gelu(x, approximate=True)

def _silu(x):
    return jax.nn.silu(x)

def _sigmoid(x):
    return jax.nn.sigmoid(x)

def _layernorm(x, axis=-1, eps=1e-05):
    m = jnp.mean(x, axis=axis, keepdims=True)
    v = jnp.var(x, axis=axis, keepdims=True)
    return (x - m) / jnp.sqrt(v + eps)

def _scatter_add(tgt, idx, src, axis=0):
    return tgt.at[idx].add(src)

def _segment_sum(src, seg, n):
    return jax.ops.segment_sum(src, seg, n)
kernel_name = 'mk_macaron_d1_jaxref_r4_f91575'

def setup_inputs(seed: int=0):
    np.random.seed(seed)
    _w = jnp.asarray

    def _L0_attn_setup():
        import jax, jax.numpy as jnp
        import numpy as np
        N_EMBD = 256
        N_HEAD = 16
        HEAD_DIM = N_EMBD // N_HEAD
        KV_RANK = 64
        Q_RANK = 128
        ROPE_DIM = 32
        B, T = (2, 512)
        EPS = 1e-06

        def _rope_tables(T, dim):
            inv_freq = 1.0 / 10000.0 ** (np.arange(0, dim, 2, dtype=np.float32) / dim)
            t = np.arange(T, dtype=np.float32)
            freqs = np.outer(t, inv_freq)
            emb = np.concatenate([freqs, freqs], -1)
            return (jnp.asarray(np.cos(emb)), jnp.asarray(np.sin(emb)))

        def _apply_rope(x, cos, sin):
            d2 = x.shape[-1] // 2
            x1, x2 = (x[..., :d2], x[..., d2:])
            rot = jnp.concatenate([-x2, x1], axis=-1)
            return x * cos[None, None, :, :] + rot * sin[None, None, :, :]
        key = jax.random.key(seed)
        ks = jax.random.split(key, 10)

        def w(k, fan_in, fan_out):
            return jax.random.normal(k, (fan_in, fan_out), dtype=jnp.float32) * fan_in ** (-0.5)
        return {'x': jax.random.normal(ks[0], (B, T, N_EMBD), dtype=jnp.float32), 'W_kv': w(ks[1], N_EMBD, KV_RANK), 'g_kv': jnp.ones((KV_RANK,), dtype=jnp.float32), 'W_kdec': w(ks[2], KV_RANK, N_HEAD * HEAD_DIM), 'W_vdec': w(ks[3], KV_RANK, N_HEAD * HEAD_DIM), 'W_q': w(ks[4], N_EMBD, Q_RANK), 'W_qdec': w(ks[5], Q_RANK, N_HEAD * HEAD_DIM), 'W_krope': w(ks[6], N_EMBD, N_HEAD * ROPE_DIM), 'W_qrope': w(ks[7], Q_RANK, N_HEAD * ROPE_DIM), 'W_o': w(ks[8], N_HEAD * HEAD_DIM, N_EMBD)}
    _L0_attn_in = _L0_attn_setup()

    def _L0_ffn_setup():
        import jax, jax.numpy as jnp
        import numpy as np
        TOP_K = 2
        EPS = 1e-06
        key = jax.random.key(seed)
        ks = jax.random.split(key, 6)
        B_, T, D = (8, 512, 256)
        E, R_ = (8, 16)
        scale = 1.0 / np.sqrt(D)
        x = jax.random.normal(ks[0], (B_, T, D), dtype=jnp.float32)
        W = jax.random.normal(ks[1], (D, D), dtype=jnp.float32) * scale
        b = jax.random.normal(ks[2], (D,), dtype=jnp.float32)
        R = jax.random.normal(ks[3], (E, D), dtype=jnp.float32) * scale
        A = jax.random.normal(ks[4], (E, R_, D), dtype=jnp.float32) * scale
        B = jax.random.normal(ks[5], (D, R_), dtype=jnp.float32)[None] * jnp.ones((E, 1, 1), jnp.float32)
        B = jax.random.normal(ks[5], (E, D, R_), dtype=jnp.float32) * (1.0 / np.sqrt(R_))
        return {'x': x, 'W': W, 'b': b, 'R': R, 'A': A, 'B': B}
    _L0_ffn_in = _L0_ffn_setup()
    _d = {'L0_attn_x': _L0_attn_in['x'], 'L0_attn_W_kv': _L0_attn_in['W_kv'], 'L0_attn_g_kv': _L0_attn_in['g_kv'], 'L0_attn_W_kdec': _L0_attn_in['W_kdec'], 'L0_attn_W_vdec': _L0_attn_in['W_vdec'], 'L0_attn_W_q': _L0_attn_in['W_q'], 'L0_attn_W_qdec': _L0_attn_in['W_qdec'], 'L0_attn_W_krope': _L0_attn_in['W_krope'], 'L0_attn_W_qrope': _L0_attn_in['W_qrope'], 'L0_attn_W_o': _L0_attn_in['W_o'], 'L0_ffn_W': _L0_ffn_in['W'], 'L0_ffn_b': _L0_ffn_in['b'], 'L0_ffn_R': _L0_ffn_in['R'], 'L0_ffn_A': _L0_ffn_in['A'], 'L0_ffn_B': _L0_ffn_in['B']}
    _x0 = _d['L0_attn_x']
    _d['L0_attn_x'] = jax.random.normal(jax.random.fold_in(jax.random.key(seed), 1), (8, 1024, 256), dtype=_x0.dtype)
    del _x0
    return _d

def reference(L0_attn_x, L0_attn_W_kv, L0_attn_g_kv, L0_attn_W_kdec, L0_attn_W_vdec, L0_attn_W_q, L0_attn_W_qdec, L0_attn_W_krope, L0_attn_W_qrope, L0_attn_W_o, L0_ffn_W, L0_ffn_b, L0_ffn_R, L0_ffn_A, L0_ffn_B):

    def _L0_attn_ref(x, W_kv, g_kv, W_kdec, W_vdec, W_q, W_qdec, W_krope, W_qrope, W_o):
        import jax, jax.numpy as jnp
        import numpy as np
        N_EMBD = 256
        N_HEAD = 16
        HEAD_DIM = N_EMBD // N_HEAD
        KV_RANK = 64
        Q_RANK = 128
        ROPE_DIM = 32
        B, T = (2, 512)
        EPS = 1e-06

        def _rope_tables(T, dim):
            inv_freq = 1.0 / 10000.0 ** (np.arange(0, dim, 2, dtype=np.float32) / dim)
            t = np.arange(T, dtype=np.float32)
            freqs = np.outer(t, inv_freq)
            emb = np.concatenate([freqs, freqs], -1)
            return (jnp.asarray(np.cos(emb)), jnp.asarray(np.sin(emb)))

        def _apply_rope(x, cos, sin):
            d2 = x.shape[-1] // 2
            x1, x2 = (x[..., :d2], x[..., d2:])
            rot = jnp.concatenate([-x2, x1], axis=-1)
            return x * cos[None, None, :, :] + rot * sin[None, None, :, :]
        Bx, Tx, C = x.shape
        kv_c = x @ W_kv
        kv_c = kv_c * jax.lax.rsqrt(jnp.mean(kv_c * kv_c, axis=-1, keepdims=True) + EPS) * g_kv
        q_c = x @ W_q

        def heads(y, d):
            return y.reshape(Bx, Tx, N_HEAD, d).transpose(0, 2, 1, 3)
        k_content = heads(kv_c @ W_kdec, HEAD_DIM)
        v = heads(kv_c @ W_vdec, HEAD_DIM)
        q_content = heads(q_c @ W_qdec, HEAD_DIM)
        k_rope = heads(x @ W_krope, ROPE_DIM)
        q_rope = heads(q_c @ W_qrope, ROPE_DIM)
        cos, sin = _rope_tables(Tx, ROPE_DIM)
        q_rope = _apply_rope(q_rope, cos, sin)
        k_rope = _apply_rope(k_rope, cos, sin)
        q = jnp.concatenate([q_content, q_rope], axis=-1)
        k = jnp.concatenate([k_content, k_rope], axis=-1)
        scale = 1.0 / jnp.sqrt(jnp.float32(q.shape[-1]))
        scores = jnp.einsum('bhqd,bhkd->bhqk', q, k) * scale
        causal = jnp.tril(jnp.ones((Tx, Tx), dtype=bool))
        scores = jnp.where(causal[None, None], scores, jnp.float32(-jnp.inf))
        attn = jax.nn.softmax(scores, axis=-1)
        out = jnp.einsum('bhqk,bhkd->bhqd', attn, v)
        out = out.transpose(0, 2, 1, 3).reshape(Bx, Tx, N_HEAD * HEAD_DIM)
        return out @ W_o

    def _L0_ffn_ref(x, W, b, R, A, B):
        import jax, jax.numpy as jnp
        import numpy as np
        TOP_K = 2
        EPS = 1e-06
        base_out = jnp.einsum('btd,od->bto', x, W) + b
        logits = jnp.einsum('btd,ed->bte', x, R)
        gate = jax.nn.softmax(logits, axis=-1)
        E = gate.shape[-1]
        _, idx = jax.lax.top_k(gate, TOP_K)
        mask = jax.nn.one_hot(idx, E, dtype=gate.dtype).sum(axis=-2)
        gate = gate * mask
        gate = gate / (gate.sum(axis=-1, keepdims=True) + EPS)
        h = jnp.einsum('btd,erd->bter', x, A)
        gh = gate[..., None] * h
        lora_out = jnp.einsum('bter,eor->bto', gh, B)
        return base_out + lora_out
    x = L0_attn_x
    x = x + 0.5 * _L0_ffn_ref(_layernorm(x, axis=-1), L0_ffn_W, L0_ffn_b, L0_ffn_R, L0_ffn_A, L0_ffn_B)
    x = x + _L0_attn_ref(_layernorm(x, axis=-1), L0_attn_W_kv, L0_attn_g_kv, L0_attn_W_kdec, L0_attn_W_vdec, L0_attn_W_q, L0_attn_W_qdec, L0_attn_W_krope, L0_attn_W_qrope, L0_attn_W_o)
    x = x + 0.5 * _L0_ffn_ref(_layernorm(x, axis=-1), L0_ffn_W, L0_ffn_b, L0_ffn_R, L0_ffn_A, L0_ffn_B)
    return x

_drawn_inputs = setup_inputs


def setup_inputs(seed=0):
    import zlib

    import numpy as np

    out = dict(_drawn_inputs(seed))
    spreads = {'L0_attn_g_kv': (1.0, 0.2)}
    factors = {}
    for name, (base, spread) in spreads.items():
        noise = np.random.default_rng([zlib.crc32(name.encode()), seed]).standard_normal(out[name].shape)
        drawn = base * np.exp(spread * noise) if base else spread * noise
        out[name] = jnp.asarray(drawn.astype(out[name].dtype))
    for name, factor in factors.items():
        out[name] = (out[name] * factor).astype(out[name].dtype)
    return out
```

```python
from contextlib import ExitStack

import concourse.bass as bass
from concourse import mybir

F32 = mybir.dt.float32
F32R = mybir.dt.float32r
BF16 = mybir.dt.bfloat16
U32 = mybir.dt.uint32
ALU = mybir.AluOpType
ACT = mybir.ActivationFunctionType
AX_X = mybir.AxisListType.X

P = 128
B, T, D = 8, 1024, 256
H, DC, DR, DV = 16, 16, 32, 16
DQ = DC + DR
QR, KR = 128, 64
E, R = 8, 16
ER = E * R
KD = D // P
TB = T // P
HQ = 4
NQ = H // HQ
GT = 4
HALF = 512

PQ, PKR, PKC, PV_ = 0, HQ * DQ, HQ * DQ + HQ * DR, HQ * DQ + HQ * DR + HQ * DC
HLW = ER + E
STGW = 3 * P + 1
LN_EPS, RMS_EPS, GATE_EPS = 1e-5, 1e-6, 1e-6
NEG = -3.0e38
SCALE = float(DQ) ** -0.5

ATT = []
for h2 in range(T // HALF):
    for j in range((h2 + 1) * HALF // P):
        q0 = max(P * j, HALF * h2)
        ATT.append((h2, j, q0, HALF * (h2 + 1) - q0, q0 == P * j))
NS = len(ATT)
UNITS = NS * HQ
DIAG = [s for s in range(NS) if ATT[s][4]]
HALF_END = [max(s for s in range(NS) if ATT[s][0] == h2) for h2 in range(2)]

MXC = []
for a in range(HQ):
    for i in range(TB):
        for c in range(2):
            k0, k1 = HALF * c, min(HALF * (c + 1), P * (i + 1))
            if k1 > k0:
                MXC.append((a, i, c, k0, k1 - k0, k1 == P * (i + 1)))
NM = len(MXC)

def pieces(base):
    out = []
    for a in range(HQ):
        f, r = base + DQ * a, 0
        while r < DQ:
            n = min(DQ - r, P - (f + r) % P)
            out.append((a, r, (f + r) // P, (f + r) % P, n))
            r += n
    return out


Q_PIECES, K_PIECES = pieces(0), pieces(HQ * DQ)
HI_PER_HEAD = [sum(1 for p in Q_PIECES + K_PIECES if p[0] == a) for a in range(HQ)]
N_REST = len(Q_PIECES) + 3 * len(K_PIECES)

JOB_A, JOB_C = "before attention", "after attention"
USES = {JOB_A: 12, JOB_C: 9}
RT = 9


def plan(att, mx, proj, job, tail, load_cur):
    at = [[] for _ in range(UNITS)]

    def put(u, *step):
        at[u].append(step)

    if load_cur:
        put(0, "load_cur")
    if mx:
        put(0, "stacks")
    if tail:
        put(0, "o_out", 1)
    if job:
        put(0, "x_load")
    for s in range(NS if att else 0):
        for a in range(HQ):
            put(HQ * s + a, "score", s, a)
        if s:
            put(HQ * s + 1, "pv", s - 1)
    if att:
        put(UNITS - 1, "pv", NS - 1)
        put(HQ * (HALF_END[0] + 1) + 2, "o_out", 0)
    if mx:
        first, last = 5, 42
        for m in range(NM):
            put(first + m * (last - first) // NM, "mx", m)
        put(last, "mx_fold")
        put(last + 1, "mx_turn")
        put(last + 2, "shift")
    if proj:
        for t in range(TB):
            put(17 + 3 * t, "proj", t)
            put(19 + 3 * t, "turn", t)
    if job:
        c = job == JOB_C
        u = 3
        if c:
            put(3, "wo", 0)
            put(5, "wo", 1)
            u = 6
        put(u, "stats", 0)
        put(u + 1, "norm", 0)
        put(u + 3, "tr", 0)
        put(u + 5, "tr", 1)
        put(u + 7, "low", 0)
        put(u + 9, "low", 1)
        for k in range(RT):
            put(u + 10 + k, "route", k)
        put(u + 20, "gated")
        put(u + 22, "gated_tr")
        put(u + 24, "y", 0)
        put(u + 26, "y", 1)
        put(u + 27, "x_store")
        if not c:
            put(u + 27, "stats", 1)
            put(u + 28, "norm", 1)
            put(u + 30, "tr2", 0)
            put(u + 32, "tr2", 1)
            put(u + 34, "qc")
            put(u + 36, "kv")
            put(u + 38, "ss")
            put(u + 39, "nx_store")
    return [step for unit in at for step in unit]


def first(t, g):
    return isinstance(t.g, int) and t.g == g


def first_turn(t):
    return first(t, 0)


def first_mx(t):
    return first(t, -1)


def first_proj(t):
    return first(t, -2)


def no_mx_before(t):
    return first(t, -1) or first(t, -2)


def i_par(k):
    return k % 2


class Turn:

    def __init__(self, b, q, att=True, mx=True, proj=True, job=None, tail=True, J=0, w=0, JA=0, JC=0, prev=None):
        self.b, self.q, self.g = b, q, NQ * b + q
        self.att, self.mx, self.proj, self.job, self.tail = att, mx, proj, job, tail
        self.J, self.w, self.JA, self.JC, self.prev = J, w, JA, JC, prev
        self.load_cur = proj and q == 2
        self.steps = plan(att, mx, proj, job, tail, self.load_cur)


def turns_before():
    none = dict(att=False, mx=False, proj=False, tail=False)
    return [
        Turn(-1, 0, **none, job=JOB_A, J=0, w=0, JA=0),
        Turn(-1, 1, **none, job=JOB_A, J=1, w=12, JA=1, prev=JOB_A),
        Turn(-1, 2, att=False, mx=False, tail=False),
        Turn(-1, 3, att=False, tail=False),
    ]


def turns_of(b, first=False, last=False):
    if first:
        J, w = 2, 24
    elif last:
        J, w = 4 * b - 2, 48 + 42 * (b - 1) - 24
    else:
        J, w = 4 * b, 48 + 42 * (b - 1)
    out = []
    for q in range(NQ):
        a = q < 2
        job = None if (a and last) or (not a and first) else (JOB_A if a else JOB_C)
        prev = JOB_A if (first or 0 < q < 3) else JOB_C
        if last and q == 2:
            prev = JOB_C
        out.append(Turn(b, q, mx=not (last and q == 3), proj=not (last and q >= 2), job=job,
                        tail=not (first and q == 0), J=J + q, w=w + (12 * q if a else 24 + 9 * (q - 2)),
                        JA=2 * (b + 1) + q, JC=2 * (b - 1) + q - 2, prev=prev))
    return out


def turns_after():
    none = dict(att=False, mx=False, proj=False)
    w = 48 + 42 * (B - 2) + 18
    return [
        Turn(B, 0, **none, tail=True, job=JOB_C, J=4 * B - 2, w=w, JC=2 * (B - 1), prev=JOB_C),
        Turn(B, 1, **none, tail=False, job=JOB_C, J=4 * B - 1, w=w + 9, JC=2 * B - 1, prev=JOB_C),
    ]


def build(nc, x, w1, bt, bias, wkvq, wkr, wkv, g_kv, wq, wo, cos, sin, out):
    with ExitStack() as ctx:
        def sb(name, shape, dt=F32):
            return ctx.enter_context(nc.sbuf_tensor(name, shape, dt))

        def bank(name, n=1):
            return ctx.enter_context(nc.psum_tensor(name, [P, n, HALF], F32))

        def sem(name):
            return ctx.enter_context(nc.semaphore(name))

        x1_d = nc.dram_tensor("x1_scratch", (2 * B, P, GT, D), F32).ap()
        nx_d = nc.dram_tensor("nx_scratch", (2, P, GT, STGW), F32).ap()
        kv_d = nc.dram_tensor("kv_scratch", (2, KR, GT, P), F32).ap()
        sh_d = nc.dram_tensor("shift_scratch", (2, HQ * TB, P), F32).ap()
        ao_d = nc.dram_tensor("ao_scratch", (B, D, T), F32).ap()
        x_g = x.rearrange("(g t p) d -> g p t d", t=GT, p=P)
        out_g = out.rearrange("(g t p) d -> g p t d", t=GT, p=P)

        ident = sb("ident", [P, P])
        ones = sb("ones", [P, 2])
        tick = sb("tick", [P, 8])
        tri = sb("tri", [P, HALF], BF16)
        iota = sb("iota", [P, E])
        powers = sb("powers", [P, GT])
        w1_s = sb("w1_s", [P, KD, D + HLW])
        bt_s = sb("bt_s", [P, D])
        hb_s = sb("hb_s", [P, D])
        wkvq_s = sb("wkvq_s", [P, KD, KR + QR])
        wkr_s = sb("wkr_s", [P, KD, NQ, HQ * DR])
        wkv_s = sb("wkv_s", [KR, NQ, 2 * HQ * DC])
        wq_s = sb("wq_s", [P, NQ, HQ * DQ])
        wo_s = sb("wo_s", [P, KD, D])
        cos_s = sb("cos_s", [P, TB, DR])
        sin_s = sb("sin_s", [P, TB, DR])
        g_s = sb("g_s", [KR, 1])

        q_st = [sb(f"q_st{i}", [P, HQ, T], F32R) for i in range(2)]
        k1_st = [sb(f"k1_st{i}", [P, HQ, T], F32R) for i in range(2)]
        k2_st = [sb(f"k2_st{i}", [P, HQ, T], F32R) for i in range(2)]
        src_hi = sb("src_hi", [P, 3, T], F32R)
        src_lo = sb("src_lo", [P, 3, T], F32R)
        v_s = [sb(f"v_s{i}", [P, TB, HQ, DV + 1]) for i in range(NQ)]
        probs = sb("probs", [P, 2, HQ, HALF])
        mx_s = sb("mx_s", [P, HQ * TB, 2])
        mxf = sb("mxf", [P, HQ * TB])
        shift = sb("shift", [HQ * TB, P], F32R)
        o_t = sb("o_t", [P, HALF // 32, 32])
        o_rc = sb("o_rc", [P, HALF // 32, 1])
        o_f = sb("o_f", [P, HALF])
        qk = sb("qk", [P, 2, 2 * HQ, DQ])
        rot_c = sb("rot_c", [P, 2 * HQ, DR])
        rot_s = sb("rot_s", [P, 2 * HQ, DR])
        cur = sb("cur", [P, TB, STGW])
        kvc = sb("kvc", [KR, TB, P])

        xa = sb("xa", [P, GT, D])
        xn = sb("xn", [P, GT, D])
        gh = xn[:, 0:2, :].rearrange("p a (t k) -> p (a t) k", k=ER)
        ght = xn[:, 2:4, :].rearrange("p a k -> p (a k)")
        xt = sb("xt", [P, GT, KD, P])
        hl = sb("hl", [P, GT, HLW])
        stg = sb("stg", [P, GT, STGW])
        kvs = sb("kvs", [KR, GT, P])
        ksq = sb("ksq", [KR, GT * P])
        aoc = sb("aoc", [P, KD, GT * P])
        bst = sb("bst", [P, GT, 6])
        mv = sb("mv", [P, GT, 2])
        ve = sb("ve", [P, GT])
        rs = sb("rs", [P, GT])
        ssv = sb("ssv", [P, GT])
        m8 = sb("m8", [P, GT, E])
        ix = sb("ix", [P, GT, E], U32)
        ixf = sb("ixf", [P, GT, 2])
        ls = sb("ls", [P, GT, E])
        ex = sb("ex", [P, GT, E])
        k1m = sb("k1m", [P, GT, E])
        k2m = sb("k2m", [P, GT, E])
        msk = sb("msk", [P, GT, E])
        em = sb("em", [P, GT, E])
        se = sb("se", [P, GT])
        sm = sb("sm", [P, GT])
        den = sb("den", [P, GT])
        rc = sb("rc", [P, GT])
        gate = sb("gate", [P, GT, E])

        st_b = bank("st_b", 2)
        mx_b = bank("mx_b", 2)
        o_b = bank("o_b")
        wp_b = bank("wp_b")
        tp_b = bank("tp_b")
        wj_b = bank("wj_b")

        w_in = sem("w_in")
        const = sem("const")
        prep = sem("prep")
        x_in, ao_in = sem("x_in"), sem("ao_in")
        stored, nx_out, ao_out = sem("stored"), sem("nx_out"), sem("ao_out")
        cur_in = sem("cur_in")
        hi_in = [sem(f"hi_in{a}") for a in range(HQ)]
        rest_in, shift_in, shift_out = sem("rest_in"), sem("shift_in"), sem("shift_out")
        st_full, exp_done, masked = sem("st_full"), sem("exp_done"), sem("masked")
        pv_done, o_read, o_rcp, o_nrm, o_ready = (sem("pv_done"), sem("o_read"), sem("o_rcp"), sem("o_nrm"),
                                                  sem("o_ready"))
        mx_full, mx_done, mx_folded = sem("mx_full"), sem("mx_done"), sem("mx_folded")
        mx_turned, shift_ready = sem("mx_turned"), sem("shift_ready")
        wp_full, wp_read, roped, rot1 = sem("wp_full"), sem("wp_read"), sem("roped"), sem("rot1")
        tp_full, hi_done, lo_done = sem("tp_full"), sem("hi_done"), sem("lo_done")
        wj_full, wj_free = sem("wj_full"), sem("wj_free")
        stat1 = [sem("stat1_0"), sem("stat1_1")]
        stat2 = [sem("stat2_0"), sem("stat2_1")]
        rv = [sem("rv_0"), sem("rv_1")]
        rstd = [sem("rstd_0"), sem("rstd_1")]
        normed = [sem("normed_0"), sem("normed_1")]
        biased = sem("biased")
        rt = sem("rt")
        exped = sem("exped")
        rcd, gates, gated = sem("rcd"), sem("gates"), sem("gated")
        ss_read, r_done = sem("ss_read"), sem("r_done")

        N_W = 11
        block = ctx.enter_context(nc.Block())

        def walk(eng, turn):
            for t in turns_before() + turns_of(0, first=True):
                turn(t)
            with eng.Fori(1, B - 1) as b:
                for t in turns_of(b):
                    turn(t)
            for t in turns_of(B - 1, last=True) + turns_after():
                turn(t)

        def stand_dve(c):
            nc.vector.tensor_copy(tick[:, c:c + 1], ones[:, 0:1])

        def stand_pool(c):
            nc.gpsimd.tensor_tensor(tick[:, c:c + 1], powers[:, 0:1], powers[:, 1:2], ALU.add)

        def f32(tensor):
            return tensor[:, :, :].bitcast(F32) if len(tensor.shape) == 3 else tensor[:, :].bitcast(F32)

        def job_use(t, name, k):
            order = ["tr0", "tr1", "low0", "low1", "gated_tr0", "y0", "y1"]
            if t.job == JOB_A:
                order += ["tr20", "tr21", "qc0", "kv0", "ss0"]
            else:
                order = ["wo0", "wo1"] + order
            return t.w + order.index(f"{name}{k}")

        @block.sync
        def _(sp):
            sp.dma_start(w1_s[:, :, :], w1.rearrange("(k p) n -> p k n", p=P)).then_inc(w_in, 16)
            sp.dma_start(bt_s[:, :], bt).then_inc(w_in, 16)
            sp.dma_start(hb_s[:, :], bias.rearrange("(a n) -> a n", a=1).to_broadcast([P, D])).then_inc(w_in, 16)
            sp.dma_start(wkvq_s[:, :, :], wkvq.rearrange("(k p) n -> p k n", p=P)).then_inc(w_in, 16)
            sp.dma_start(wkr_s[:, :, :, :], wkr.rearrange("(k p) q n -> p k q n", p=P)).then_inc(w_in, 16)
            sp.dma_start(wkv_s[:, :, :], wkv).then_inc(w_in, 16)
            sp.dma_start(g_s[:, :], g_kv).then_inc(w_in, 16)
            sp.dma_start(wq_s[:, :, :], wq).then_inc(w_in, 16)
            sp.dma_start(wo_s[:, :, :], wo.rearrange("(k p) n -> p k n", p=P)).then_inc(w_in, 16)
            sp.dma_start(cos_s[:, :, :], cos).then_inc(w_in, 16)
            sp.dma_start(sin_s[:, :, :], sin).then_inc(w_in, 16)

            def turn(t):
                g, b, q = t.g, t.b, t.q
                u = q % 2
                for name, *arg in t.steps:
                    if name == "x_load":
                        if t.prev is not None:
                            sp.wait_ge(stored, 16 * t.J)
                        if t.prev == JOB_A:
                            sp.wait_ge(normed[1], t.JA if t.job == JOB_A else 2 * b + 4)
                        if t.job == JOB_A:
                            sp.dma_start(xa[:, :, :], x_g[t.JA]).then_inc(x_in, 16)
                        else:
                            sp.dma_start(xa[:, :, :], x1_d[t.JC]).then_inc(x_in, 16)
                            sp.wait_ge(ao_out, 128 * NQ * b)
                            sp.wait_ge(wj_full, t.w)
                            half = t.q % 2
                            bb = b - 1
                            sp.dma_start(aoc[:, :, :], ao_d[bb].rearrange("(k p) t -> p k t", p=P)[
                                :, :, GT * P * half:GT * P * (half + 1)]).then_inc(ao_in, 16)
                    elif name == "x_store":
                        sp.wait_ge(wj_free, job_use(t, "y", 1) + 1)
                        if t.job == JOB_A:
                            sp.dma_start(x1_d[t.JA], xa[:, :, :]).then_inc(stored, 16)
                        else:
                            sp.dma_start(out_g[t.JC], xa[:, :, :]).then_inc(stored, 16)
                    elif name == "nx_store":
                        sp.wait_ge(r_done, t.JA + 1)
                        sp.wait_ge(wj_free, job_use(t, "kv", 0) + 1)
                        if not (isinstance(b, int) and b < 0):
                            sp.wait_ge(cur_in, 32 * (b + 1))
                        sp.dma_start(nx_d[q], stg[:, :, :]).then_inc(nx_out, 16)
                        sp.dma_start(kv_d[q], kvs[:, :, :]).then_inc(nx_out, 16)
                    elif name == "load_cur":
                        sp.wait_ge(nx_out, 64 * (b + 2))
                        if not (isinstance(b, int) and b < 0):
                            sp.wait_ge(wp_full, TB * NQ * (b + 1))
                            sp.wait_ge(wp_read, TB * NQ * (b + 1))
                        sp.dma_start(cur[:, :, :].rearrange("p (h t) n -> p h t n", h=2),
                                     nx_d.rearrange("h p t n -> p h t n")).then_inc(cur_in, 16)
                        sp.dma_start(kvc[:, :, :].rearrange("p (h t) n -> p h t n", h=2),
                                     kv_d.rearrange("h p t n -> p h t n")).then_inc(cur_in, 16)
                    elif name == "stacks":
                        v = (q + 1) % 2
                        sp.wait_ge(hi_done, TB * (g + 2))
                        sp.wait_ge(lo_done, TB * (g + 2))
                        if t.tail:
                            sp.wait_ge(pv_done, NS * g)
                        qs, k1, k2 = f32(q_st[v]), f32(k1_st[v]), f32(k2_st[v])
                        hi, lo = f32(src_hi), f32(src_lo)
                        for a in range(HQ):
                            for dst, ps in ((qs, Q_PIECES), (k1, K_PIECES)):
                                for pa, r, c, p0, n in ps:
                                    if pa == a:
                                        sp.dma_start(dst[r:r + n, a, :], hi[p0:p0 + n, c, :]).then_inc(hi_in[a], 16)
                        for dst, src, off, ps in ((k1, lo, DQ, K_PIECES), (qs, lo, DQ, Q_PIECES),
                                                  (k2, lo, 0, K_PIECES), (k2, hi, DQ, K_PIECES)):
                            for a, r, c, p0, n in ps:
                                sp.dma_start(dst[off + r:off + r + n, a, :],
                                             src[p0:p0 + n, c, :]).then_inc(rest_in, 16)
                    elif name == "shift":
                        sp.wait_ge(shift_ready, g + 2)
                        v = (q + 1) % 2
                        sp.dma_start(sh_d[v], f32(shift)).then_inc(shift_out, 16)
                        sp.wait_ge(shift_out, 16 * (g + 2))
                        sp.dma_start(f32(q_st[v])[2 * DQ:2 * DQ + 1, :, :].rearrange("o a t -> o (a t)"),
                                     sh_d[v].rearrange("i c -> (i c)").unsqueeze(0)).then_inc(shift_in, 16)
                    elif name == "o_out":
                        h2 = arg[0]
                        gg = g if h2 == 0 else g - 1
                        bb, qq = (b, q) if h2 == 0 else (b, q - 1) if q else (b - 1, NQ - 1)
                        sp.wait_ge(o_ready, 2 * gg + h2 + 1)
                        for a in range(HQ):
                            row = HQ * DV * qq + DV * a
                            sp.dma_start(ao_d[bb][row:row + DV, HALF * h2:HALF * (h2 + 1)],
                                         o_f[32 * a:32 * a + DV, :]).then_inc(ao_out, 16)

            walk(sp, turn)
            sp.wait_ge(stored, 16 * 4 * B)
            sp.wait_ge(nx_out, 64 * B)
            sp.wait_ge(ao_out, 128 * NQ * B)

        @block.tensor
        def _(pe):
            pe.wait_ge(w_in, 16 * N_W)
            pe.wait_ge(const, 10)
            pe.wait_ge(prep, 2)

            def turn(t):
                g, b, q = t.g, t.b, t.q
                u = q % 2
                for name, *arg in t.steps:
                    if name == "score":
                        s, a = arg
                        h2, j, q0, n, _ = ATT[s]
                        i = UNITS * g + HQ * s + a
                        if s == 0 and a == 0:
                            pe.wait_ge(shift_in, 16 * (g + 1))
                            pe.wait_ge(rest_in, 16 * N_REST * (g + 1))
                        if not (first_turn(t) and HQ * s + a < 2):
                            pe.wait_ge(exp_done, i - 1)
                        dst = st_b[:, a % 2, 0:n]
                        nc.tensor.matmul(dst, k1_st[u][0:2 * DQ + 1, a, P * j:P * j + P],
                                         q_st[u][0:2 * DQ + 1, a, q0:q0 + n], start=True, stop=False)
                        nc.tensor.matmul(dst, k2_st[u][0:2 * DQ, a, P * j:P * j + P],
                                         q_st[u][0:2 * DQ, a, q0:q0 + n], start=False, stop=True).then_inc(st_full, 1)
                    elif name == "pv":
                        s = arg[0]
                        h2, j, q0, n, diag = ATT[s]
                        if diag:
                            pe.wait_ge(masked, len(DIAG) * g + DIAG.index(s) + 1)
                        else:
                            pe.wait_ge(exp_done, UNITS * g + HQ * (s + 1))
                        if j == 0 and not (first_turn(t) and h2 == 0):
                            pe.wait_ge(o_read, 2 * g + h2)
                        for a in range(HQ):
                            last = nc.tensor.matmul(o_b[32 * a:32 * a + DV + 1, 0, q0 - HALF * h2:q0 - HALF * h2 + n],
                                                    v_s[q][:, j, a, :], probs[:, s % 2, a, 0:n],
                                                    start=(j == 0), stop=(s in HALF_END))
                        last.then_inc(pv_done, 1)
                    elif name == "mx":
                        m = arg[0]
                        a, i, c, k0, n, _ = MXC[m]
                        v = (q + 1) % 2
                        if m == 0 or MXC[m - 1][0] != a:
                            pe.wait_ge(hi_in[a], 16 * HI_PER_HEAD[a] * (g + 2))
                        if not (first_mx(t) and m < 2):
                            pe.wait_ge(mx_done, NM * (g + 1) + m - 1)
                        nc.tensor.matmul(mx_b[:, m % 2, 0:n], q_st[v][0:DQ, a, P * i:P * i + P],
                                         k1_st[v][0:DQ, a, k0:k0 + n], start=True, stop=True).then_inc(mx_full, 1)
                    elif name == "mx_turn":
                        pe.wait_ge(mx_folded, g + 2)
                        if t.proj:
                            pe.wait_ge(lo_done, TB * (g + 3))
                        elif not first_mx(t):
                            pe.wait_ge(shift_ready, g + 1)
                        nc.tensor.transpose(tp_b[0:HQ * TB, 0, 3 * P:4 * P], mxf[:, :], ident[:, :]).then_inc(mx_turned, 1)
                    elif name == "proj":
                        k = arg[0]
                        i = TB * (g + 2) + k
                        r = (q + 2) % NQ
                        if k == 0:
                            pe.wait_ge(cur_in, 32 * (b + 1 if q < 2 else b + 2))
                        if not (first_proj(t) and k == 0):
                            pe.wait_ge(wp_read, i)
                        nc.tensor.matmul(wp_b[:, 0, PQ:PKR], cur[:, k, 2 * P:3 * P], wq_s[:, r, :],
                                         start=True, stop=True)
                        for kk in range(KD):
                            nc.tensor.matmul(wp_b[:, 0, PKR:PKC], cur[:, k, kk * P:(kk + 1) * P], wkr_s[:, kk, r, :],
                                             start=(kk == 0), stop=(kk == KD - 1))
                        nc.tensor.matmul(wp_b[:, 0, PKC:PKC + 2 * HQ * DC], kvc[:, k, :], wkv_s[:, r, :],
                                         start=True, stop=True).then_inc(wp_full, 1)
                    elif name == "turn":
                        k = arg[0]
                        i = TB * (g + 2) + k
                        pe.wait_ge(roped, i + 1)
                        if not (first_proj(t) and k == 0):
                            pe.wait_ge(lo_done, i)
                        if k == 0 and not first_proj(t) and not no_mx_before(t):
                            pe.wait_ge(shift_ready, g + 1)
                        flat = qk[:, i_par(k), :, :].rearrange("p h c -> p (h c)")
                        for c in range(3):
                            last = nc.tensor.transpose(tp_b[:, 0, P * c:P * c + P], flat[:, P * c:P * c + P], ident[:, :])
                        last.then_inc(tp_full, 1)
                    elif name in ("wo", "tr", "low", "gated_tr", "y", "tr2", "qc", "kv", "ss"):
                        k = arg[0] if arg else 0
                        w = job_use(t, name, k)
                        if not (isinstance(w, int) and w == 0):
                            pe.wait_ge(wj_free, w)
                        wj = wj_b[:, 0, :]
                        if name == "wo":
                            if k == 0:
                                pe.wait_ge(ao_in, 16 * (t.JC + 1))
                            for tt in range(2):
                                for kk in range(KD):
                                    tk = 2 * k + tt
                                    last = nc.tensor.matmul(wj[:, D * tt:D * tt + D], aoc[:, kk, P * tk:P * tk + P],
                                                            wo_s[:, kk, :], start=(kk == 0), stop=(kk == KD - 1))
                        elif name in ("tr", "tr2"):
                            if k == 0:
                                n = t.J if name == "tr" else t.JA
                                pe.wait_ge(normed[name == "tr2"], n + 1)
                            for tt in range(2):
                                for kk in range(KD):
                                    c = KD * tt + kk
                                    last = nc.tensor.transpose(wj[:, P * c:P * c + P],
                                                               xn[:, 2 * k + tt, P * kk:P * kk + P], ident[:, :])
                        elif name == "low":
                            for tt in range(2):
                                for kk in range(KD):
                                    last = nc.tensor.matmul(wj[:, HLW * tt:HLW * tt + HLW], xt[:, 2 * k + tt, kk, :],
                                                            w1_s[:, kk, D:D + HLW], start=(kk == 0), stop=(kk == KD - 1))
                        elif name == "gated_tr":
                            pe.wait_ge(gated, t.J + 1)
                            for tk in range(GT):
                                last = nc.tensor.transpose(wj[:, P * tk:P * tk + P], gh[:, tk, :], ident[:, :])
                        elif name == "y":
                            for tt in range(2):
                                tk = 2 * k + tt
                                dst = wj[:, D * tt:D * tt + D]
                                for kk in range(KD):
                                    nc.tensor.matmul(dst, xt[:, tk, kk, :], w1_s[:, kk, 0:D], start=(kk == 0), stop=False)
                                last = nc.tensor.matmul(dst, ght[:, P * tk:P * tk + P], bt_s[:, :], start=False, stop=True)
                        elif name == "qc":
                            for kk in range(KD):
                                last = nc.tensor.matmul(wj[:, :].rearrange("p (t c) -> p t c", c=P),
                                                        wkvq_s[:, kk, KR:KR + QR],
                                                        stg[:, :, kk * P:(kk + 1) * P], start=(kk == 0), stop=(kk == KD - 1))
                        elif name == "kv":
                            for kk in range(KD):
                                last = nc.tensor.matmul(wj[0:KR, :].rearrange("p (t c) -> p t c", c=P),
                                                        wkvq_s[:, kk, 0:KR],
                                                        stg[:, :, kk * P:(kk + 1) * P], start=(kk == 0), stop=(kk == KD - 1))
                        elif name == "ss":
                            for tk in range(GT):
                                last = nc.tensor.matmul(wj[:, tk:tk + 1], ksq[:, P * tk:P * tk + P], ones[0:KR, 0:1],
                                                        start=True, stop=True)
                        last.then_inc(wj_full, 1)

            walk(pe, turn)

        @block.scalar
        def _(act):
            act.wait_ge(const, 10)

            def turn(t):
                g, b, q = t.g, t.b, t.q
                for name, *arg in t.steps:
                    if name == "score":
                        s, a = arg
                        n = ATT[s][3]
                        act.wait_ge(st_full, UNITS * g + HQ * s + a + 1)
                        if a == 0 and not (first_turn(t) and s < 2):
                            act.wait_ge(pv_done, NS * g + s - 1)
                        nc.scalar.activation(probs[:, s % 2, a, 0:n], st_b[:, a % 2, 0:n], ACT.Exp,
                                             scale=SCALE).then_inc(exp_done, 1)
                    elif name == "proj":
                        k = arg[0]
                        i = TB * (g + 2) + k
                        r = (q + 2) % NQ
                        act.wait_ge(wp_full, i + 1)
                        if not (first_proj(t) and k < 2):
                            act.wait_ge(tp_full, i - 1)
                        d = qk[:, i_par(k), :, :]
                        src = wp_b[:, 0, :]
                        rms = cur[:, k, 3 * P:3 * P + 1]
                        nc.scalar.activation(d[:, 0:HQ, :], src[:, PQ:PKR].rearrange("p (a c) -> p a c", c=DQ), ACT.Copy)
                        nc.scalar.activation(d[:, HQ:2 * HQ, DC:DQ],
                                             src[:, PKR:PKC].rearrange("p (a c) -> p a c", c=DR), ACT.Copy)
                        nc.scalar.activation(d[:, HQ:2 * HQ, 0:DC],
                                             src[:, PKC:PV_].rearrange("p (a c) -> p a c", c=DC), ACT.Copy, scale=rms)
                        nc.scalar.activation(v_s[r][:, k, :, 0:DV],
                                             src[:, PV_:PV_ + HQ * DV].rearrange("p (a c) -> p a c", c=DV), ACT.Copy,
                                             scale=rms).then_inc(wp_read, 1)
                    elif name == "turn":
                        k = arg[0]
                        i = TB * (g + 2) + k
                        act.wait_ge(tp_full, i + 1)
                        if k == 0 and t.mx:
                            for a in range(HQ):
                                act.wait_ge(hi_in[a], 16 * HI_PER_HEAD[a] * (g + 2))
                            act.wait_ge(rest_in, 16 * N_REST * (g + 2))
                        nc.scalar.activation(src_hi[:, :, P * k:P * k + P],
                                             tp_b[:, 0, 0:3 * P].rearrange("p (c n) -> p c n", n=P),
                                             ACT.Copy).then_inc(hi_done, 1)
                    elif name in ("tr", "low", "gated_tr", "tr2", "qc", "kv"):
                        k = arg[0] if arg else 0
                        act.wait_ge(wj_full, job_use(t, name, k) + 1)
                        wj = wj_b[:, 0, :]
                        if name == "tr":
                            dst, src = xt[:, 2 * k:2 * k + 2, :, :].rearrange("p t k n -> p (t k n)"), wj
                        elif name == "low":
                            dst = hl[:, 2 * k:2 * k + 2, :].rearrange("p t n -> p (t n)")
                            src = wj[:, 0:2 * HLW]
                        elif name == "gated_tr":
                            dst, src = ght, wj
                        elif name == "tr2":
                            if k == 0 and not (isinstance(t.JA, int) and t.JA == 0):
                                act.wait_ge(nx_out, 32 * t.JA)
                            dst = stg[:, 2 * k:2 * k + 2, 0:2 * P]
                            src = wj.rearrange("p (t n) -> p t n", n=2 * P)
                        elif name == "qc":
                            dst, src = stg[:, :, 2 * P:3 * P], wj.rearrange("p (t n) -> p t n", n=P)
                        elif name == "kv":
                            nc.scalar.activation(kvs[:, :, :].rearrange("p t n -> p (t n)"), wj[0:KR, :], ACT.Copy)
                            dst, src = ksq[:, :], wj[0:KR, :]
                        nc.scalar.activation(dst, src, ACT.Square if name == "kv" else ACT.Copy).then_inc(wj_free, 1)
                    elif name == "route" and arg[0] == 3:
                        act.wait_ge(rt, RT * t.J + 3)
                        nc.scalar.activation(ex[:, :, :], ls[:, :, :], ACT.Exp).then_inc(exped, 1)

            walk(act, turn)

        @block.vector
        def _(dve):
            nc.vector.memset(o_b[:, :, :], 0.0).then_inc(const, 1)
            nc.vector.memset(mx_s[:, :, :], NEG).then_inc(const, 1)
            for i in range(2):
                nc.vector.memset(f32(k1_st[i])[2 * DQ:2 * DQ + 1, :, :], 1.0)
            nc.vector.memset(ones[:, :], 1.0).then_inc(const, 1)
            dve.wait_ge(w_in, 16 * N_W)
            nc.vector.tensor_scalar(hb_s[:, :], hb_s[:, :], 0.5, None, ALU.mult).then_inc(prep, 1)
            nc.vector.tensor_scalar(wkv_s[:, :, :], wkv_s[:, :, :], g_s[:, 0:1], None, ALU.mult).then_inc(prep, 1)
            dve.wait_ge(prep, 2)
            dve.wait_ge(const, 10)

            def turn(t):
                g, b, q = t.g, t.b, t.q
                for name, *arg in t.steps:
                    if name == "mx":
                        m = arg[0]
                        a, i, c, k0, n, diag = MXC[m]
                        dve.wait_ge(mx_full, NM * (g + 1) + m + 1)
                        if diag:
                            stand_dve(m % 2)
                        src = mx_b[:, m % 2, 0:n]
                        dst = mx_s[:, TB * a + i, c:c + 1]
                        if diag:
                            nc.vector.tensor_tensor_reduce(src, src, tri[:, HALF - n:HALF], 1.0, NEG, ALU.add,
                                                           ALU.max, dst).then_inc(mx_done, 1)
                        else:
                            nc.vector.tensor_reduce(dst, src, AX_X, ALU.max).then_inc(mx_done, 1)
                    elif name == "mx_fold":
                        dve.wait_ge(mx_done, NM * (g + 2))
                        if not first_mx(t):
                            dve.wait_ge(mx_turned, g + 1)
                        nc.vector.tensor_reduce(mxf[:, :], mx_s[:, :, :], AX_X, ALU.max).then_inc(mx_folded, 1)
                    elif name == "mx_turn":
                        dve.wait_ge(mx_turned, g + 2)
                        if not first_mx(t):
                            dve.wait_ge(shift_in, 16 * (g + 1))
                        nc.vector.tensor_scalar(shift[:, :], tp_b[0:HQ * TB, 0, 3 * P:4 * P], -1.0, None,
                                                ALU.mult).then_inc(shift_ready, 1)
                    elif name == "o_out":
                        h2 = arg[0]
                        gg = g if h2 == 0 else g - 1
                        n = 2 * gg + h2
                        dve.wait_ge(pv_done, NS * gg + HALF_END[h2] + 1)
                        nc.vector.transpose(o_t[:, :, :].rearrange("p a c -> p (a c)"), o_b[:, 0, :]).then_inc(o_read, 1)
                        dve.wait_ge(o_read, n + 1)
                        nc.vector.reciprocal(o_rc[:, :, :], o_t[:, :, DV:DV + 1]).then_inc(o_rcp, 1)
                        dve.wait_ge(o_rcp, n + 1)
                        nc.vector.tensor_tensor(o_t[:, :, 0:DV], o_t[:, :, 0:DV],
                                                o_rc[:, :, :].to_broadcast([P, HALF // 32, DV]),
                                                ALU.mult).then_inc(o_nrm, 1)
                        dve.wait_ge(o_nrm, n + 1)
                        if not (isinstance(n, int) and n == 0):
                            dve.wait_ge(ao_out, 64 * n)
                        nc.vector.transpose(o_f[:, :], o_t[:, :, :].rearrange("p a c -> p (a c)")).then_inc(o_ready, 1)
                    elif name == "turn":
                        k = arg[0]
                        i = TB * (g + 2) + k
                        dve.wait_ge(hi_done, i + 1)
                        nc.vector.tensor_tensor(src_lo[:, :, P * k:P * k + P],
                                                tp_b[:, 0, 0:3 * P].rearrange("p (c n) -> p c n", n=P),
                                                f32(src_hi)[:, :, P * k:P * k + P],
                                                ALU.subtract).then_inc(lo_done, 1)
                    elif name == "wo":
                        k = arg[0]
                        if k == 0:
                            dve.wait_ge(x_in, 16 * (t.J + 1))
                        dve.wait_ge(wj_full, job_use(t, name, k) + 1)
                        d = xa[:, 2 * k:2 * k + 2, :].rearrange("p t n -> p (t n)")
                        nc.vector.tensor_tensor(d, wj_b[:, 0, :], d, ALU.add).then_inc(wj_free, 1)
                    elif name == "stats":
                        k = arg[0]
                        n = t.JA if k else t.J
                        if k:
                            dve.wait_ge(wj_free, job_use(t, "y", 1) + 1)
                        elif t.job == JOB_A:
                            dve.wait_ge(x_in, 16 * (t.J + 1))
                        else:
                            dve.wait_ge(wj_free, job_use(t, "wo", 1) + 1)
                        for tk in range(GT):
                            last = nc.vector.bn_stats(bst[:, tk, :], xa[:, tk, :])
                        last.then_inc(stat1[k], 1)
                        dve.wait_ge(stat1[k], n + 1)
                        stand_dve(2)
                        for tk in range(GT):
                            last = nc.vector.bn_aggr(mv[:, tk, :], bst[:, tk, :])
                        last.then_inc(stat2[k], 1)
                    elif name == "norm":
                        k = arg[0]
                        n = t.JA if k else t.J
                        dve.wait_ge(rstd[k], n + 1)
                        for tk in range(GT):
                            last = nc.vector.tensor_scalar(xn[:, tk, :], xa[:, tk, :], mv[:, tk, 0:1], rs[:, tk:tk + 1],
                                                           ALU.subtract, ALU.mult)
                        last.then_inc(normed[k], 1)
                    elif name == "route":
                        k = arg[0]
                        n = RT * t.J
                        if k == 0:
                            dve.wait_ge(wj_free, job_use(t, "low", 1) + 1)
                            stand_dve(3)
                            for tk in range(GT):
                                last = nc.vector.max(m8[:, tk, :], hl[:, tk, ER:HLW])
                            last.then_inc(rt, 1)
                        elif k == 1:
                            dve.wait_ge(rt, n + 1)
                            stand_dve(4)
                            for tk in range(GT):
                                last = nc.vector.max_index(ix[:, tk, :], m8[:, tk, :], hl[:, tk, ER:HLW])
                            last.then_inc(rt, 1)
                        elif k == 2:
                            nc.vector.tensor_tensor(ls[:, :, :], hl[:, :, ER:HLW],
                                                    m8[:, :, 0:1].to_broadcast([P, GT, E]), ALU.subtract).then_inc(rt, 1)
                        elif k == 3:
                            dve.wait_ge(rt, n + 2)
                            nc.vector.tensor_copy(ixf[:, :, :], ix[:, :, 0:2]).then_inc(rt, 1)
                        elif k == 4:
                            dve.wait_ge(rt, n + 4)
                            io = iota[:, :].unsqueeze(1).to_broadcast([P, GT, E])
                            nc.vector.tensor_tensor(k1m[:, :, :], io, ixf[:, :, 0:1].to_broadcast([P, GT, E]), ALU.is_equal)
                            nc.vector.tensor_tensor(k2m[:, :, :], io, ixf[:, :, 1:2].to_broadcast([P, GT, E]),
                                                    ALU.is_equal).then_inc(rt, 1)
                        elif k == 5:
                            dve.wait_ge(rt, n + 5)
                            dve.wait_ge(exped, t.J + 1)
                            nc.vector.tensor_tensor(msk[:, :, :], k1m[:, :, :], k2m[:, :, :], ALU.add)
                            nc.vector.tensor_reduce(se[:, :], ex[:, :, :], AX_X, ALU.add).then_inc(rt, 1)
                        elif k == 6:
                            dve.wait_ge(rt, n + 6)
                            nc.vector.tensor_tensor(em[:, :, :], ex[:, :, :], msk[:, :, :], ALU.mult).then_inc(rt, 1)
                        elif k == 7:
                            dve.wait_ge(rt, n + 7)
                            nc.vector.tensor_reduce(sm[:, :], em[:, :, :], AX_X, ALU.add).then_inc(rt, 1)
                        elif k == 8:
                            dve.wait_ge(rt, n + 8)
                            nc.vector.scalar_tensor_tensor(out=den[:, :], in0=se[:, :], scalar=GATE_EPS, in1=sm[:, :],
                                                           op0=ALU.mult, op1=ALU.add).then_inc(rt, 1)
                    elif name == "gated":
                        dve.wait_ge(rt, RT * t.J + 9)
                        nc.vector.reciprocal(rc[:, :], den[:, :]).then_inc(rcd, 1)
                        dve.wait_ge(rcd, t.J + 1)
                        nc.vector.tensor_tensor(gate[:, :, :], em[:, :, :],
                                                rc[:, :].unsqueeze(2).to_broadcast([P, GT, E]), ALU.mult).then_inc(gates, 1)
                    elif name == "y":
                        k = arg[0]
                        if k == 0:
                            dve.wait_ge(biased, t.J + 1)
                        dve.wait_ge(wj_full, job_use(t, name, k) + 1)
                        d = xa[:, 2 * k:2 * k + 2, :].rearrange("p t n -> p (t n)")
                        nc.vector.scalar_tensor_tensor(out=d, in0=wj_b[:, 0, :], scalar=0.5, in1=d, op0=ALU.mult,
                                                       op1=ALU.add).then_inc(wj_free, 1)
                    elif name == "ss":
                        dve.wait_ge(wj_full, job_use(t, name, 0) + 1)
                        nc.vector.tensor_scalar(ssv[:, :], wj_b[:, 0, 0:GT], 1.0 / KR, RMS_EPS, ALU.mult,
                                                ALU.add).then_inc(wj_free, 1)

            walk(dve, turn)

        @block.gpsimd
        def _(pool):
            nc.gpsimd.memset(ident[:, :], 0.0).then_inc(const, 1)
            nc.gpsimd.memset(tri[:, :], 0.0).then_inc(const, 1)
            nc.gpsimd.memset(powers[:, :], -0.5).then_inc(const, 1)
            nc.gpsimd.iota(iota[:, :], pattern=[[1, E]], base=0, channel_multiplier=0,
                           allow_small_or_imprecise_dtypes=True).then_inc(const, 1)
            for i in range(NQ):
                last = nc.gpsimd.memset(v_s[i][:, :, :, :], 1.0)
            last.then_inc(const, 1)
            pool.wait_ge(const, 8)
            nc.gpsimd.affine_select(out=ident[:, :], in_=ident[:, :], compare_op=ALU.not_equal, fill=1.0, base=0,
                                    pattern=[[-1, P]], channel_multiplier=1).then_inc(const, 1)
            nc.gpsimd.affine_select(out=tri[:, HALF - P:HALF], in_=tri[:, HALF - P:HALF], compare_op=ALU.is_ge,
                                    fill=-1.0e38, base=0, pattern=[[-1, P]], channel_multiplier=1).then_inc(const, 1)
            pool.wait_ge(const, 10)
            pool.wait_ge(w_in, 16 * N_W)
            pool.wait_ge(prep, 2)

            def turn(t):
                g, b, q = t.g, t.b, t.q
                for name, *arg in t.steps:
                    if name == "score" and arg[1] == HQ - 1 and ATT[arg[0]][4]:
                        s = arg[0]
                        pool.wait_ge(exp_done, UNITS * g + HQ * (s + 1))
                        stand_pool(5)
                        d = probs[:, s % 2, :, 0:P]
                        nc.gpsimd.affine_select(out=d, in_=d, compare_op=ALU.is_ge, fill=0.0, base=0,
                                                pattern=[[0, HQ], [1, P]], channel_multiplier=-1).then_inc(masked, 1)
                    elif name == "proj":
                        k = arg[0]
                        i = TB * (g + 2) + k
                        pool.wait_ge(wp_read, i + 1)
                        d = qk[:, i_par(k), :, :]
                        cs = cos_s[:, k, :].unsqueeze(1).to_broadcast([P, 2 * HQ, DR])
                        sn = sin_s[:, k, :].unsqueeze(1).to_broadcast([P, 2 * HQ, DR])
                        hd = DR // 2
                        nc.gpsimd.tensor_tensor(rot_c[:, :, :], d[:, :, DC:DQ], cs, ALU.mult)
                        nc.gpsimd.tensor_tensor(rot_s[:, :, 0:hd], d[:, :, DC + hd:DQ], sn[:, :, 0:hd], ALU.mult)
                        nc.gpsimd.tensor_tensor(rot_s[:, :, hd:DR], d[:, :, DC:DC + hd], sn[:, :, hd:DR],
                                                ALU.mult).then_inc(rot1, 1)
                        pool.wait_ge(rot1, i + 1)
                        nc.gpsimd.tensor_tensor(d[:, :, DC:DQ], rot_c[:, :, :], rot_s[:, :, :],
                                                ALU.add).then_inc(roped, 1)
                    elif name == "stats":
                        k = arg[0]
                        n = t.JA if k else t.J
                        pool.wait_ge(stat2[k], n + 1)
                        stand_pool(6)
                        nc.gpsimd.tensor_scalar(ve[:, :], mv[:, :, 1], LN_EPS, None, ALU.add).then_inc(rv[k], 1)
                        pool.wait_ge(rv[k], n + 1)
                        nc.gpsimd.tensor_tensor(rs[:, :], ve[:, :], powers[:, :], ALU.pow).then_inc(rstd[k], 1)
                    elif name == "norm" and arg[0] == 0:
                        pool.wait_ge(normed[0], t.J + 1)
                        nc.gpsimd.tensor_tensor(xa[:, :, :], xa[:, :, :],
                                                hb_s[:, :].unsqueeze(1).to_broadcast([P, GT, D]),
                                                ALU.add).then_inc(biased, 1)
                    elif name == "gated":
                        pool.wait_ge(gates, t.J + 1)
                        nc.gpsimd.tensor_tensor(gh.rearrange("p t (e r) -> p t e r", r=R),
                                                hl[:, :, 0:ER].rearrange("p t (e r) -> p t e r", r=R),
                                                gate[:, :, :].unsqueeze(3).to_broadcast([P, GT, E, R]),
                                                ALU.mult).then_inc(gated, 1)
                    elif name == "ss":
                        pool.wait_ge(wj_free, job_use(t, name, 0) + 1)
                        nc.gpsimd.tensor_tensor(stg[:, :, 3 * P], ssv[:, :], powers[:, :], ALU.pow).then_inc(r_done, 1)

            walk(pool, turn)


def kernel(L0_attn_x, L0_attn_W_kv, L0_attn_g_kv, L0_attn_W_kdec, L0_attn_W_vdec, L0_attn_W_q, L0_attn_W_qdec,
           L0_attn_W_krope, L0_attn_W_qrope, L0_attn_W_o, L0_ffn_W, L0_ffn_b, L0_ffn_R, L0_ffn_A, L0_ffn_B):
    import numpy as np
    import concourse.bacc as bacc
    from concourse.bass_utils import run_bass_kernel_spmd

    a = np.asarray
    inv_freq = 1.0 / 10000.0 ** (np.arange(0, DR, 2, dtype=np.float32) / DR)
    freqs = np.outer(np.arange(T, dtype=np.float32), inv_freq)
    emb = np.concatenate([freqs, freqs], -1)
    cos, sin = np.cos(emb), np.sin(emb)
    sin[:, :DR // 2] *= -1
    per_quad = lambda w, n: a(w).reshape(-1, NQ, HQ, n)
    arrays = {
        "x": a(L0_attn_x).reshape(B * T, D),
        "w1": np.concatenate([a(L0_ffn_W).T, a(L0_ffn_A).reshape(ER, D).T, a(L0_ffn_R).T], 1),
        "bt": a(L0_ffn_B).transpose(0, 2, 1).reshape(ER, D),
        "bias": a(L0_ffn_b),
        "wkvq": np.concatenate([a(L0_attn_W_kv), a(L0_attn_W_q)], 1),
        "wkr": a(L0_attn_W_krope).reshape(D, NQ, HQ * DR),
        "wkv": np.concatenate([a(L0_attn_W_kdec).reshape(KR, NQ, HQ * DC),
                               a(L0_attn_W_vdec).reshape(KR, NQ, HQ * DV)], 2),
        "g_kv": a(L0_attn_g_kv).reshape(KR, 1),
        "wq": np.concatenate([per_quad(L0_attn_W_qdec, DC), per_quad(L0_attn_W_qrope, DR)],
                             3).reshape(QR, NQ, HQ * DQ),
        "wo": a(L0_attn_W_o),
        "cos": cos.astype(np.float32).reshape(TB, P, DR).transpose(1, 0, 2),
        "sin": sin.astype(np.float32).reshape(TB, P, DR).transpose(1, 0, 2),
    }
    arrays = {"in_" + k: np.ascontiguousarray(v) for k, v in arrays.items()}
    nc = bacc.Bacc("TRN2", target_bir_lowering=False, num_devices=1, dynamic_dma_scratch_size=1024)
    args = [nc.dram_tensor(k, v.shape, F32, kind="ExternalInput").ap() for k, v in arrays.items()]
    out = nc.dram_tensor("out_y", (B * T, D), F32, kind="ExternalOutput").ap()
    nc.disable_value_cache = True
    build(nc, *args, out)
    r = run_bass_kernel_spmd(nc, [arrays], core_ids=[0])
    return r.results[0]["out_y"].reshape(B, T, D)
```

```python
from contextlib import ExitStack

import concourse.bass as bass
from concourse import mybir

F32 = mybir.dt.float32
F32R = mybir.dt.float32r
BF16 = mybir.dt.bfloat16
U32 = mybir.dt.uint32
ALU = mybir.AluOpType
ACT = mybir.ActivationFunctionType
AX_X = mybir.AxisListType.X

P = 128
B, T, D = 8, 1024, 256
H, DC, DR, DV = 16, 16, 32, 16
DQ = DC + DR
QR, KR = 128, 64
E, R = 8, 16
ER = E * R
KD = D // P
TB = T // P
HQ = 4
NQ = H // HQ
GT = 4
HALF = 512

PQ, PKR, PKC, PV_ = 0, HQ * DQ, HQ * DQ + HQ * DR, HQ * DQ + HQ * DR + HQ * DC
HLW = ER + E
STGW = 3 * P + 1
LN_EPS, RMS_EPS, GATE_EPS = 1e-5, 1e-6, 1e-6
NEG = -3.0e38
SCALE = float(DQ) ** -0.5

ATT = []
for h2 in range(T // HALF):
    for j in range((h2 + 1) * HALF // P):
        q0 = max(P * j, HALF * h2)
        ATT.append((h2, j, q0, HALF * (h2 + 1) - q0, q0 == P * j))
NS = len(ATT)
UNITS = NS * HQ
DIAG = [s for s in range(NS) if ATT[s][4]]
HALF_END = [max(s for s in range(NS) if ATT[s][0] == h2) for h2 in range(2)]

MXC = []
for i in range(TB):
    for a in range(HQ):
        for c in range(2):
            k0, k1 = HALF * c, min(HALF * (c + 1), P * (i + 1))
            if k1 > k0:
                MXC.append((a, i, c, k0, k1 - k0, k1 == P * (i + 1)))
NM = len(MXC)

ODD = 64
SHIFT = ODD + DQ
HT = TB // 2

JOB_A, JOB_C = "before attention", "after attention"
USES = {JOB_A: 12, JOB_C: 9}
RT = 9


def mx_steps(i):
    return [m for m in range(NM) if MXC[m][1] == i]


def plan(att, proj, job, tail, load_cur):
    at = [[] for _ in range(UNITS)]

    def put(u, *step):
        at[min(u, UNITS - 1)].append(step)

    if tail:
        put(1 if att else 0, "o_out", 1)
    if job:
        put(0, "x_load")
    for s in range(NS if att else 0):
        for a in range(HQ):
            put(HQ * s + a, "score", s, a)
        if s:
            put(HQ * s + 1, "pv", s - 1)
    if att:
        put(UNITS - 1, "pv", NS - 1)
        put(HQ * (HALF_END[0] + 1) + 2, "o_out", 0)
    if proj:
        for t in range(TB):
            u = 1 + 33 * t // (TB - 1)
            put(u, "proj", t)
            put(u + 4, "turn", t)
            ms = mx_steps(t)
            for n, m in enumerate(ms):
                put(u + 7 + 5 * n // len(ms), "mx", m)
            if t % HT == HT - 1:
                put(u + 5, "k2", t // HT)
                put(u + 12, "mx_fold", t // HT)
                put(u + 13, "mx_turn", t // HT)
                put(u + 14, "shift", t // HT)
    if load_cur:
        put(40, "load_cur")
    if job:
        c = job == JOB_C
        u = 4
        if c:
            put(5, "wo", 0)
            put(7, "wo", 1)
            u = 8
        put(u, "stats", 0)
        put(u + 1, "norm", 0)
        put(u + 3, "tr", 0)
        put(u + 5, "tr", 1)
        put(u + 7, "low", 0)
        put(u + 9, "low", 1)
        for k in range(RT):
            put(u + 10 + k, "route", k)
        put(u + 20, "gated")
        put(u + 22, "gated_tr")
        put(u + 24, "y", 0)
        put(u + 26, "y", 1)
        put(u + 27, "x_store")
        if not c:
            put(u + 27, "stats", 1)
            put(u + 28, "norm", 1)
            put(u + 30, "tr2", 0)
            put(u + 32, "tr2", 1)
            put(u + 34, "qc")
            put(u + 36, "kv")
            put(u + 38, "ss")
            put(u + 39, "nx_store")
    return [step for unit in at for step in unit]


TP_USES = [(n, a[0]) for n, *a in plan(True, True, None, True, False) if n in ("turn", "mx_turn")]


def tp_use(t, name, k):
    return len(TP_USES) * (t.g + 1) + TP_USES.index((name, k))


def zero(n):
    return isinstance(n, int) and n == 0


def first(t, g):
    return isinstance(t.g, int) and t.g == g


def first_turn(t):
    return first(t, 0)


def first_proj(t):
    return first(t, -1)


def i_par(k):
    return k % 2


class Turn:

    def __init__(self, b, q, att=True, proj=True, load_cur=None, job=None, tail=True, J=0, w=0, JA=0, JC=0, prev=None):
        self.b, self.q, self.g = b, q, NQ * b + q
        self.att, self.proj, self.job, self.tail = att, proj, job, tail
        self.J, self.w, self.JA, self.JC, self.prev = J, w, JA, JC, prev
        self.load_cur = q == 2 if load_cur is None else load_cur
        self.steps = plan(att, proj, job, tail, self.load_cur)


def turns_before():
    none = dict(att=False, proj=False, tail=False)
    return [
        Turn(-1, 0, **none, job=JOB_A, J=0, w=0, JA=0),
        Turn(-1, 1, **none, job=JOB_A, J=1, w=12, JA=1, prev=JOB_A),
        Turn(-1, 2, **none),
        Turn(-1, 3, att=False, tail=False),
    ]


def turns_of(b, first=False, last=False):
    if first:
        J, w = 2, 24
    elif last:
        J, w = 4 * b - 2, 48 + 42 * (b - 1) - 24
    else:
        J, w = 4 * b, 48 + 42 * (b - 1)
    out = []
    for q in range(NQ):
        a = q < 2
        job = None if (a and last) or (not a and first) else (JOB_A if a else JOB_C)
        prev = JOB_A if (first or 0 < q < 3) else JOB_C
        if last and q == 2:
            prev = JOB_C
        out.append(Turn(b, q, proj=not (last and q == 3), load_cur=q == 2 and not last, job=job,
                        tail=not (first and q == 0), J=J + q, w=w + (12 * q if a else 24 + 9 * (q - 2)),
                        JA=2 * (b + 1) + q, JC=2 * (b - 1) + q - 2, prev=prev))
    return out


def turns_after():
    none = dict(att=False, proj=False)
    w = 48 + 42 * (B - 2) + 18
    return [
        Turn(B, 0, **none, tail=True, job=JOB_C, J=4 * B - 2, w=w, JC=2 * (B - 1), prev=JOB_C),
        Turn(B, 1, **none, tail=False, job=JOB_C, J=4 * B - 1, w=w + 9, JC=2 * B - 1, prev=JOB_C),
    ]


def build(nc, x, w1, bt, bias, wkvq, wkr, wkv, g_kv, wq, wo, cos, sin, out):
    with ExitStack() as ctx:
        def sb(name, shape, dt=F32):
            return ctx.enter_context(nc.sbuf_tensor(name, shape, dt))

        def bank(name, n=1):
            return ctx.enter_context(nc.psum_tensor(name, [P, n, HALF], F32))

        def sem(name):
            return ctx.enter_context(nc.semaphore(name))

        x1_d = nc.dram_tensor("x1_scratch", (2 * B, P, GT, D), F32).ap()
        nx_d = nc.dram_tensor("nx_scratch", (2, P, GT, STGW), F32).ap()
        kv_d = nc.dram_tensor("kv_scratch", (2, KR, GT, P), F32).ap()
        sh_d = nc.dram_tensor("shift_scratch", (2, HQ * HT, P), F32).ap()
        ao_d = nc.dram_tensor("ao_scratch", (B, D, T), F32).ap()
        x_g = x.rearrange("(g t p) d -> g p t d", t=GT, p=P)
        out_g = out.rearrange("(g t p) d -> g p t d", t=GT, p=P)

        ident = sb("ident", [P, P])
        ones = sb("ones", [P, 2])
        tick = sb("tick", [P, 8])
        tri = sb("tri", [P, HALF], BF16)
        iota = sb("iota", [P, E])
        powers = sb("powers", [P, GT])
        w1_s = sb("w1_s", [P, KD, D + HLW])
        bt_s = sb("bt_s", [P, D])
        hb_s = sb("hb_s", [P, D])
        wkvq_s = sb("wkvq_s", [P, KD, KR + QR])
        wkr_s = sb("wkr_s", [P, KD, NQ, HQ * DR])
        wkv_s = sb("wkv_s", [KR, NQ, 2 * HQ * DC])
        wq_s = sb("wq_s", [P, NQ, HQ * DQ])
        wo_s = sb("wo_s", [P, KD, D])
        cos_s = sb("cos_s", [P, TB, DR])
        sin_s = sb("sin_s", [P, TB, DR])
        g_s = sb("g_s", [KR, 1])

        st = [sb(f"st{i}", [P, 2, HQ, T], F32R) for i in range(2)]
        k2_st = [sb(f"k2_st{i}", [P, HQ, T], F32R) for i in range(2)]
        q_st = [s[:, 0] for s in st]
        k1_st = [s[:, 1] for s in st]
        v_s = [sb(f"v_s{i}", [P, TB, HQ, DV + 1]) for i in range(NQ)]
        probs = sb("probs", [P, 2, HQ, HALF])
        mx_s = sb("mx_s", [P, HQ * TB, 2])
        mxf = sb("mxf", [P, HQ * TB])
        shift = sb("shift", [HQ * HT, P], F32R)
        o_t = sb("o_t", [P, HALF // 32, 32])
        o_rc = sb("o_rc", [P, HALF // 32, 1])
        o_f = sb("o_f", [P, HALF])
        qk = sb("qk", [P, 2, 2 * HQ, ODD])
        rot_c = sb("rot_c", [P, 2 * HQ, DR])
        rot_s = sb("rot_s", [P, 2 * HQ, DR])
        cur = sb("cur", [P, TB, STGW])
        kvc = sb("kvc", [KR, TB, P])

        xa = sb("xa", [P, GT, D])
        xn = sb("xn", [P, GT, D])
        gh = xn[:, 0:2, :].rearrange("p a (t k) -> p (a t) k", k=ER)
        ght = xn[:, 2:4, :].rearrange("p a k -> p (a k)")
        xt = sb("xt", [P, GT, KD, P])
        hl = sb("hl", [P, GT, HLW])
        stg = sb("stg", [P, GT, STGW])
        kvs = sb("kvs", [KR, GT, P])
        ksq = sb("ksq", [KR, GT * P])
        aoc = sb("aoc", [P, KD, GT * P])
        bst = sb("bst", [P, GT, 6])
        mv = sb("mv", [P, GT, 2])
        ve = sb("ve", [P, GT])
        rs = sb("rs", [P, GT])
        ssv = sb("ssv", [P, GT])
        m8 = sb("m8", [P, GT, E])
        ix = sb("ix", [P, GT, E], U32)
        ixf = sb("ixf", [P, GT, 2])
        ls = sb("ls", [P, GT, E])
        ex = sb("ex", [P, GT, E])
        k1m = sb("k1m", [P, GT, E])
        k2m = sb("k2m", [P, GT, E])
        msk = sb("msk", [P, GT, E])
        em = sb("em", [P, GT, E])
        se = sb("se", [P, GT])
        sm = sb("sm", [P, GT])
        den = sb("den", [P, GT])
        rc = sb("rc", [P, GT])
        gate = sb("gate", [P, GT, E])

        st_b = bank("st_b", 2)
        mx_b = bank("mx_b", 2)
        o_b = bank("o_b")
        wp_b = bank("wp_b")
        tp_b = bank("tp_b")
        wj_b = bank("wj_b")

        w_in = sem("w_in")
        const = sem("const")
        prep = sem("prep")
        x_in, ao_in = sem("x_in"), sem("ao_in")
        stored, nx_out, ao_out = sem("stored"), sem("nx_out"), sem("ao_out")
        cur_in = sem("cur_in")
        k2_in, shift_in, shift_out = sem("k2_in"), sem("shift_in"), sem("shift_out")
        st_full, exp_done, masked = sem("st_full"), sem("exp_done"), sem("masked")
        pv_done, o_read, o_rcp, o_nrm, o_ready = (sem("pv_done"), sem("o_read"), sem("o_rcp"), sem("o_nrm"),
                                                  sem("o_ready"))
        mx_full, mx_done, mx_folded = sem("mx_full"), sem("mx_done"), sem("mx_folded")
        wp_full, wp_read, roped, rot1 = sem("wp_full"), sem("wp_read"), sem("roped"), sem("rot1")
        tp_full, hi_done, tp_free = sem("tp_full"), sem("hi_done"), sem("tp_free")
        wj_full, wj_free = sem("wj_full"), sem("wj_free")
        stat1 = [sem("stat1_0"), sem("stat1_1")]
        stat2 = [sem("stat2_0"), sem("stat2_1")]
        rv = [sem("rv_0"), sem("rv_1")]
        rstd = [sem("rstd_0"), sem("rstd_1")]
        normed = [sem("normed_0"), sem("normed_1")]
        biased = sem("biased")
        rt = sem("rt")
        exped = sem("exped")
        rcd, gates, gated = sem("rcd"), sem("gates"), sem("gated")
        ss_read, r_done = sem("ss_read"), sem("r_done")

        N_W = 11
        block = ctx.enter_context(nc.Block())

        def walk(eng, turn):
            for t in turns_before() + turns_of(0, first=True):
                turn(t)
            with eng.Fori(1, B - 1) as b:
                for t in turns_of(b):
                    turn(t)
            for t in turns_of(B - 1, last=True) + turns_after():
                turn(t)

        def stand_dve(c):
            nc.vector.tensor_copy(tick[:, c:c + 1], ones[:, 0:1])

        def stand_pool(c):
            nc.gpsimd.tensor_tensor(tick[:, c:c + 1], powers[:, 0:1], powers[:, 1:2], ALU.add)

        def f32(tensor):
            return tensor[tuple(slice(None) for _ in tensor.shape)].bitcast(F32)

        def heads(tensor, e, k):
            return tensor.rearrange("p s (y e) t -> p s y e t", e=2)[:, :, :, e, P * k:P * k + P]

        def job_use(t, name, k):
            order = ["tr0", "tr1", "low0", "low1", "gated_tr0", "y0", "y1"]
            if t.job == JOB_A:
                order += ["tr20", "tr21", "qc0", "kv0", "ss0"]
            else:
                order = ["wo0", "wo1"] + order
            return t.w + order.index(f"{name}{k}")

        @block.sync
        def _(sp):
            sp.dma_start(w1_s[:, :, :], w1.rearrange("(k p) n -> p k n", p=P)).then_inc(w_in, 16)
            sp.dma_start(bt_s[:, :], bt).then_inc(w_in, 16)
            sp.dma_start(hb_s[:, :], bias.rearrange("(a n) -> a n", a=1).to_broadcast([P, D])).then_inc(w_in, 16)
            sp.dma_start(wkvq_s[:, :, :], wkvq.rearrange("(k p) n -> p k n", p=P)).then_inc(w_in, 16)
            sp.dma_start(wkr_s[:, :, :, :], wkr.rearrange("(k p) q n -> p k q n", p=P)).then_inc(w_in, 16)
            sp.dma_start(wkv_s[:, :, :], wkv).then_inc(w_in, 16)
            sp.dma_start(g_s[:, :], g_kv).then_inc(w_in, 16)
            sp.dma_start(wq_s[:, :, :], wq).then_inc(w_in, 16)
            sp.dma_start(wo_s[:, :, :], wo.rearrange("(k p) n -> p k n", p=P)).then_inc(w_in, 16)
            sp.dma_start(cos_s[:, :, :], cos).then_inc(w_in, 16)
            sp.dma_start(sin_s[:, :, :], sin).then_inc(w_in, 16)

            def turn(t):
                g, b, q = t.g, t.b, t.q
                u = q % 2
                for name, *arg in t.steps:
                    if name == "x_load":
                        if t.prev is not None:
                            sp.wait_ge(stored, 16 * t.J)
                        if t.prev == JOB_A:
                            sp.wait_ge(normed[1], t.JA if t.job == JOB_A else 2 * b + 4)
                        if t.job == JOB_A:
                            sp.dma_start(xa[:, :, :], x_g[t.JA]).then_inc(x_in, 16)
                        else:
                            sp.dma_start(xa[:, :, :], x1_d[t.JC]).then_inc(x_in, 16)
                            sp.wait_ge(ao_out, 128 * NQ * b)
                            sp.wait_ge(wj_full, t.w)
                            half = t.q % 2
                            bb = b - 1
                            sp.dma_start(aoc[:, :, :], ao_d[bb].rearrange("(k p) t -> p k t", p=P)[
                                :, :, GT * P * half:GT * P * (half + 1)]).then_inc(ao_in, 16)
                    elif name == "x_store":
                        sp.wait_ge(wj_free, job_use(t, "y", 1) + 1)
                        if t.job == JOB_A:
                            sp.dma_start(x1_d[t.JA], xa[:, :, :]).then_inc(stored, 16)
                        else:
                            sp.dma_start(out_g[t.JC], xa[:, :, :]).then_inc(stored, 16)
                    elif name == "nx_store":
                        sp.wait_ge(r_done, t.JA + 1)
                        sp.wait_ge(wj_free, job_use(t, "kv", 0) + 1)
                        if not (isinstance(b, int) and b < 0):
                            sp.wait_ge(cur_in, 32 * (b + 1))
                        sp.dma_start(nx_d[q], stg[:, :, :]).then_inc(nx_out, 16)
                        sp.dma_start(kv_d[q], kvs[:, :, :]).then_inc(nx_out, 16)
                    elif name == "load_cur":
                        sp.wait_ge(nx_out, 64 * (b + 2))
                        if not (isinstance(b, int) and b < 0):
                            sp.wait_ge(wp_full, TB * NQ * (b + 1))
                            sp.wait_ge(wp_read, TB * NQ * (b + 1))
                        sp.dma_start(cur[:, :, :].rearrange("p (h t) n -> p h t n", h=2),
                                     nx_d.rearrange("h p t n -> p h t n")).then_inc(cur_in, 16)
                        sp.dma_start(kvc[:, :, :].rearrange("p (h t) n -> p h t n", h=2),
                                     kv_d.rearrange("h p t n -> p h t n")).then_inc(cur_in, 16)
                    elif name == "k2":
                        h2, v = arg[0], (q + 1) % 2
                        sp.wait_ge(tp_free, tp_use(t, "turn", HT * h2 + HT - 1) + 1)
                        k1, k2, cols = f32(st[v])[:, 1], f32(k2_st[v]), slice(HALF * h2, HALF * (h2 + 1))
                        sp.dma_start(k2[0:DQ, :, cols], k1[ODD:SHIFT, :, cols]).then_inc(k2_in, 16)
                        sp.dma_start(k2[ODD:SHIFT, :, cols], k1[0:DQ, :, cols]).then_inc(k2_in, 16)
                    elif name == "shift":
                        h2, v = arg[0], (q + 1) % 2
                        n = 2 * (g + 1) + h2
                        sp.wait_ge(tp_free, tp_use(t, "mx_turn", h2) + 1)
                        sp.dma_start(sh_d[h2], f32(shift)).then_inc(shift_out, 16)
                        sp.wait_ge(shift_out, 16 * (n + 1))
                        sp.dma_start(f32(st[v])[SHIFT:SHIFT + 1, 0, :, HALF * h2:HALF * (h2 + 1)],
                                     sh_d[h2].rearrange("(a i) c -> a (i c)", a=HQ).unsqueeze(0)).then_inc(shift_in, 16)
                    elif name == "o_out":
                        h2 = arg[0]
                        gg = g if h2 == 0 else g - 1
                        bb, qq = (b, q) if h2 == 0 else (b, q - 1) if q else (b - 1, NQ - 1)
                        sp.wait_ge(o_ready, 2 * gg + h2 + 1)
                        for a in range(HQ):
                            row = HQ * DV * qq + DV * a
                            sp.dma_start(ao_d[bb][row:row + DV, HALF * h2:HALF * (h2 + 1)],
                                         o_f[32 * a:32 * a + DV, :]).then_inc(ao_out, 16)

            walk(sp, turn)
            sp.wait_ge(stored, 16 * 4 * B)
            sp.wait_ge(nx_out, 64 * B)
            sp.wait_ge(ao_out, 128 * NQ * B)

        @block.tensor
        def _(pe):
            pe.wait_ge(w_in, 16 * N_W)
            pe.wait_ge(const, 10)
            pe.wait_ge(prep, 2)

            def turn(t):
                g, b, q = t.g, t.b, t.q
                u = q % 2
                for name, *arg in t.steps:
                    if name == "score":
                        s, a = arg
                        h2, j, q0, n, _ = ATT[s]
                        i = UNITS * g + HQ * s + a
                        if j == 0 and a == 0:
                            pe.wait_ge(shift_in, 16 * (2 * g + h2 + 1))
                            pe.wait_ge(k2_in, 32 * (2 * g + h2 + 1))
                        if not (first_turn(t) and HQ * s + a < 2):
                            pe.wait_ge(exp_done, i - 1)
                        dst = st_b[:, a % 2, 0:n]
                        nc.tensor.matmul(dst, k1_st[u][0:SHIFT + 1, a, P * j:P * j + P],
                                         q_st[u][0:SHIFT + 1, a, q0:q0 + n], start=True, stop=False)
                        nc.tensor.matmul(dst, k2_st[u][0:SHIFT, a, P * j:P * j + P],
                                         q_st[u][0:SHIFT, a, q0:q0 + n], start=False, stop=True).then_inc(st_full, 1)
                    elif name == "pv":
                        s = arg[0]
                        h2, j, q0, n, diag = ATT[s]
                        if diag:
                            pe.wait_ge(masked, len(DIAG) * g + DIAG.index(s) + 1)
                        else:
                            pe.wait_ge(exp_done, UNITS * g + HQ * (s + 1))
                        if j == 0 and not (first_turn(t) and h2 == 0):
                            pe.wait_ge(o_read, 2 * g + h2)
                        for a in range(HQ):
                            last = nc.tensor.matmul(o_b[32 * a:32 * a + DV + 1, 0, q0 - HALF * h2:q0 - HALF * h2 + n],
                                                    v_s[q][:, j, a, :], probs[:, s % 2, a, 0:n],
                                                    start=(j == 0), stop=(s in HALF_END))
                        last.then_inc(pv_done, 1)
                    elif name == "mx":
                        m = arg[0]
                        a, i, c, k0, n, _ = MXC[m]
                        v = (q + 1) % 2
                        if m == 0 or MXC[m - 1][1] != i:
                            pe.wait_ge(tp_free, tp_use(t, "turn", i) + 1)
                        if not (first_proj(t) and m < 2):
                            pe.wait_ge(mx_done, NM * (g + 1) + m - 1)
                        nc.tensor.matmul(mx_b[:, m % 2, 0:n], q_st[v][0:SHIFT, a, P * i:P * i + P],
                                         k1_st[v][0:SHIFT, a, k0:k0 + n], start=True, stop=True).then_inc(mx_full, 1)
                    elif name == "mx_turn":
                        h2 = arg[0]
                        pe.wait_ge(mx_folded, 2 * (g + 1) + h2 + 1)
                        pe.wait_ge(tp_free, tp_use(t, name, h2))
                        nc.tensor.transpose(tp_b[0:HQ * HT, 0, 0:P], mxf[:, HQ * HT * h2:HQ * HT * (h2 + 1)],
                                            ident[:, :]).then_inc(tp_full, 1)
                    elif name == "proj":
                        k = arg[0]
                        i = TB * (g + 1) + k
                        r = (q + 1) % NQ
                        if k == 0:
                            pe.wait_ge(cur_in, 32 * (b + 1 if q < 3 else b + 2))
                        if not (first_proj(t) and k == 0):
                            pe.wait_ge(wp_read, i)
                        nc.tensor.matmul(wp_b[:, 0, PQ:PKR], cur[:, k, 2 * P:3 * P], wq_s[:, r, :],
                                         start=True, stop=True)
                        for kk in range(KD):
                            nc.tensor.matmul(wp_b[:, 0, PKR:PKC], cur[:, k, kk * P:(kk + 1) * P], wkr_s[:, kk, r, :],
                                             start=(kk == 0), stop=(kk == KD - 1))
                        nc.tensor.matmul(wp_b[:, 0, PKC:PKC + 2 * HQ * DC], kvc[:, k, :], wkv_s[:, r, :],
                                         start=True, stop=True).then_inc(wp_full, 1)
                    elif name == "turn":
                        k = arg[0]
                        i = TB * (g + 1) + k
                        pe.wait_ge(roped, i + 1)
                        n = tp_use(t, name, k)
                        if not zero(n):
                            pe.wait_ge(tp_free, n)
                        flat = qk[:, i_par(k), :, :].rearrange("p h c -> p (h c)")
                        for c in range(HALF // P):
                            last = nc.tensor.transpose(tp_b[:, 0, P * c:P * c + P], flat[:, P * c:P * c + P], ident[:, :])
                        last.then_inc(tp_full, 1)
                    elif name in ("wo", "tr", "low", "gated_tr", "y", "tr2", "qc", "kv", "ss"):
                        k = arg[0] if arg else 0
                        w = job_use(t, name, k)
                        if not (isinstance(w, int) and w == 0):
                            pe.wait_ge(wj_free, w)
                        wj = wj_b[:, 0, :]
                        if name == "wo":
                            if k == 0:
                                pe.wait_ge(ao_in, 16 * (t.JC + 1))
                            for tt in range(2):
                                for kk in range(KD):
                                    tk = 2 * k + tt
                                    last = nc.tensor.matmul(wj[:, D * tt:D * tt + D], aoc[:, kk, P * tk:P * tk + P],
                                                            wo_s[:, kk, :], start=(kk == 0), stop=(kk == KD - 1))
                        elif name in ("tr", "tr2"):
                            if k == 0:
                                n = t.J if name == "tr" else t.JA
                                pe.wait_ge(normed[name == "tr2"], n + 1)
                            for tt in range(2):
                                for kk in range(KD):
                                    c = KD * tt + kk
                                    last = nc.tensor.transpose(wj[:, P * c:P * c + P],
                                                               xn[:, 2 * k + tt, P * kk:P * kk + P], ident[:, :])
                        elif name == "low":
                            for tt in range(2):
                                for kk in range(KD):
                                    last = nc.tensor.matmul(wj[:, HLW * tt:HLW * tt + HLW], xt[:, 2 * k + tt, kk, :],
                                                            w1_s[:, kk, D:D + HLW], start=(kk == 0), stop=(kk == KD - 1))
                        elif name == "gated_tr":
                            pe.wait_ge(gated, t.J + 1)
                            for tk in range(GT):
                                last = nc.tensor.transpose(wj[:, P * tk:P * tk + P], gh[:, tk, :], ident[:, :])
                        elif name == "y":
                            for tt in range(2):
                                tk = 2 * k + tt
                                dst = wj[:, D * tt:D * tt + D]
                                for kk in range(KD):
                                    nc.tensor.matmul(dst, xt[:, tk, kk, :], w1_s[:, kk, 0:D], start=(kk == 0), stop=False)
                                last = nc.tensor.matmul(dst, ght[:, P * tk:P * tk + P], bt_s[:, :], start=False, stop=True)
                        elif name == "qc":
                            for kk in range(KD):
                                last = nc.tensor.matmul(wj[:, :].rearrange("p (t c) -> p t c", c=P),
                                                        wkvq_s[:, kk, KR:KR + QR],
                                                        stg[:, :, kk * P:(kk + 1) * P], start=(kk == 0), stop=(kk == KD - 1))
                        elif name == "kv":
                            for kk in range(KD):
                                last = nc.tensor.matmul(wj[0:KR, :].rearrange("p (t c) -> p t c", c=P),
                                                        wkvq_s[:, kk, 0:KR],
                                                        stg[:, :, kk * P:(kk + 1) * P], start=(kk == 0), stop=(kk == KD - 1))
                        elif name == "ss":
                            for tk in range(GT):
                                last = nc.tensor.matmul(wj[:, tk:tk + 1], ksq[:, P * tk:P * tk + P], ones[0:KR, 0:1],
                                                        start=True, stop=True)
                        last.then_inc(wj_full, 1)

            walk(pe, turn)

        @block.scalar
        def _(act):
            act.wait_ge(const, 10)

            def turn(t):
                g, b, q = t.g, t.b, t.q
                for name, *arg in t.steps:
                    if name == "score":
                        s, a = arg
                        n = ATT[s][3]
                        act.wait_ge(st_full, UNITS * g + HQ * s + a + 1)
                        if a == 0 and not (first_turn(t) and s < 2):
                            act.wait_ge(pv_done, NS * g + s - 1)
                        nc.scalar.activation(probs[:, s % 2, a, 0:n], st_b[:, a % 2, 0:n], ACT.Exp,
                                             scale=SCALE).then_inc(exp_done, 1)
                    elif name == "proj":
                        k = arg[0]
                        i = TB * (g + 1) + k
                        r = (q + 1) % NQ
                        act.wait_ge(wp_full, i + 1)
                        if not (first_proj(t) and k < 2):
                            act.wait_ge(tp_full, (tp_use(t, "turn", k - 2) if k > 1 else
                                                  tp_use(t, "turn", TB - 2 + k) - len(TP_USES)) + 1)
                        d = qk[:, i_par(k), :, :]
                        src = wp_b[:, 0, :]
                        rms = cur[:, k, 3 * P:3 * P + 1]
                        nc.scalar.activation(d[:, 0:HQ, 0:DQ], src[:, PQ:PKR].rearrange("p (a c) -> p a c", c=DQ), ACT.Copy)
                        nc.scalar.activation(d[:, HQ:2 * HQ, DC:DQ],
                                             src[:, PKR:PKC].rearrange("p (a c) -> p a c", c=DR), ACT.Copy)
                        nc.scalar.activation(d[:, HQ:2 * HQ, 0:DC],
                                             src[:, PKC:PV_].rearrange("p (a c) -> p a c", c=DC), ACT.Copy, scale=rms)
                        nc.scalar.activation(v_s[r][:, k, :, 0:DV],
                                             src[:, PV_:PV_ + HQ * DV].rearrange("p (a c) -> p a c", c=DV), ACT.Copy,
                                             scale=rms).then_inc(wp_read, 1)
                    elif name == "turn":
                        k = arg[0]
                        i = TB * (g + 1) + k
                        act.wait_ge(tp_full, tp_use(t, name, k) + 1)
                        for e in range(2):
                            rows = slice(ODD * e, ODD * e + DQ)
                            nc.scalar.activation(heads(st[(q + 1) % 2][rows], e, k),
                                                 tp_b[rows, 0, :].rearrange("p (s y n) -> p s y n", s=2, n=P),
                                                 ACT.Copy).then_inc(hi_done, 1)
                    elif name in ("tr", "low", "gated_tr", "tr2", "qc", "kv"):
                        k = arg[0] if arg else 0
                        act.wait_ge(wj_full, job_use(t, name, k) + 1)
                        wj = wj_b[:, 0, :]
                        if name == "tr":
                            dst, src = xt[:, 2 * k:2 * k + 2, :, :].rearrange("p t k n -> p (t k n)"), wj
                        elif name == "low":
                            dst = hl[:, 2 * k:2 * k + 2, :].rearrange("p t n -> p (t n)")
                            src = wj[:, 0:2 * HLW]
                        elif name == "gated_tr":
                            dst, src = ght, wj
                        elif name == "tr2":
                            if k == 0 and not (isinstance(t.JA, int) and t.JA == 0):
                                act.wait_ge(nx_out, 32 * t.JA)
                            dst = stg[:, 2 * k:2 * k + 2, 0:2 * P]
                            src = wj.rearrange("p (t n) -> p t n", n=2 * P)
                        elif name == "qc":
                            dst, src = stg[:, :, 2 * P:3 * P], wj.rearrange("p (t n) -> p t n", n=P)
                        elif name == "kv":
                            nc.scalar.activation(kvs[:, :, :].rearrange("p t n -> p (t n)"), wj[0:KR, :], ACT.Copy)
                            dst, src = ksq[:, :], wj[0:KR, :]
                        nc.scalar.activation(dst, src, ACT.Square if name == "kv" else ACT.Copy).then_inc(wj_free, 1)
                    elif name == "route" and arg[0] == 3:
                        act.wait_ge(rt, RT * t.J + 3)
                        nc.scalar.activation(ex[:, :, :], ls[:, :, :], ACT.Exp).then_inc(exped, 1)

            walk(act, turn)

        @block.vector
        def _(dve):
            nc.vector.memset(o_b[:, :, :], 0.0).then_inc(const, 1)
            nc.vector.memset(mx_s[:, :, :], NEG).then_inc(const, 1)
            for i in range(2):
                nc.vector.memset(f32(st[i])[ODD - 32:ODD, :, :, :], 0.0)
                nc.vector.memset(f32(k2_st[i])[ODD - 32:ODD, :, :], 0.0)
                nc.vector.memset(f32(st[i])[P - 32:P, 1, :, :], 1.0)
            nc.vector.memset(qk[:, :, :, :], 0.0)
            nc.vector.memset(ones[:, :], 1.0).then_inc(const, 1)
            dve.wait_ge(w_in, 16 * N_W)
            nc.vector.tensor_scalar(hb_s[:, :], hb_s[:, :], 0.5, None, ALU.mult).then_inc(prep, 1)
            nc.vector.tensor_scalar(wkv_s[:, :, :], wkv_s[:, :, :], g_s[:, 0:1], None, ALU.mult).then_inc(prep, 1)
            dve.wait_ge(prep, 2)
            dve.wait_ge(const, 10)

            def turn(t):
                g, b, q = t.g, t.b, t.q
                for name, *arg in t.steps:
                    if name == "mx":
                        m = arg[0]
                        a, i, c, k0, n, diag = MXC[m]
                        dve.wait_ge(mx_full, NM * (g + 1) + m + 1)
                        if diag:
                            stand_dve(m % 2)
                        src = mx_b[:, m % 2, 0:n]
                        dst = mx_s[:, HQ * HT * (i // HT) + HT * a + i % HT, c:c + 1]
                        if diag:
                            nc.vector.tensor_tensor_reduce(src, src, tri[:, HALF - n:HALF], 1.0, NEG, ALU.add,
                                                           ALU.max, dst).then_inc(mx_done, 1)
                        else:
                            nc.vector.tensor_reduce(dst, src, AX_X, ALU.max).then_inc(mx_done, 1)
                    elif name == "mx_fold":
                        h2 = arg[0]
                        n = 2 * (g + 1) + h2
                        dve.wait_ge(mx_done, NM * (g + 1) + max(mx_steps(HT * h2 + HT - 1)) + 1)
                        rows = slice(HQ * HT * h2, HQ * HT * (h2 + 1))
                        nc.vector.tensor_reduce(mxf[:, rows], mx_s[:, rows, :], AX_X, ALU.max).then_inc(mx_folded, 1)
                    elif name == "mx_turn":
                        h2 = arg[0]
                        n = 2 * (g + 1) + h2
                        dve.wait_ge(tp_full, tp_use(t, name, h2) + 1)
                        if not zero(n):
                            dve.wait_ge(shift_in, 16 * n)
                        nc.vector.tensor_scalar(shift[:, :], tp_b[0:HQ * HT, 0, 0:P], -1.0, None,
                                                ALU.mult).then_inc(tp_free, 1)
                    elif name == "o_out":
                        h2 = arg[0]
                        gg = g if h2 == 0 else g - 1
                        n = 2 * gg + h2
                        dve.wait_ge(pv_done, NS * gg + HALF_END[h2] + 1)
                        nc.vector.transpose(o_t[:, :, :].rearrange("p a c -> p (a c)"), o_b[:, 0, :]).then_inc(o_read, 1)
                        dve.wait_ge(o_read, n + 1)
                        nc.vector.reciprocal(o_rc[:, :, :], o_t[:, :, DV:DV + 1]).then_inc(o_rcp, 1)
                        dve.wait_ge(o_rcp, n + 1)
                        nc.vector.tensor_tensor(o_t[:, :, 0:DV], o_t[:, :, 0:DV],
                                                o_rc[:, :, :].to_broadcast([P, HALF // 32, DV]),
                                                ALU.mult).then_inc(o_nrm, 1)
                        dve.wait_ge(o_nrm, n + 1)
                        if not (isinstance(n, int) and n == 0):
                            dve.wait_ge(ao_out, 64 * n)
                        nc.vector.transpose(o_f[:, :], o_t[:, :, :].rearrange("p a c -> p (a c)")).then_inc(o_ready, 1)
                    elif name == "turn":
                        k = arg[0]
                        i = TB * (g + 1) + k
                        for e in range(2):
                            dve.wait_ge(hi_done, 2 * i + e + 1)
                            rows, other = slice(ODD * e, ODD * e + DQ), slice(ODD * (1 - e), ODD * (1 - e) + DQ)
                            last = nc.vector.tensor_tensor(heads(st[(q + 1) % 2][other], e, k),
                                                    tp_b[rows, 0, :].rearrange("p (s y n) -> p s y n", s=2, n=P),
                                                    heads(f32(st[(q + 1) % 2])[rows], e, k), ALU.subtract)
                        last.then_inc(tp_free, 1)
                    elif name == "wo":
                        k = arg[0]
                        if k == 0:
                            dve.wait_ge(x_in, 16 * (t.J + 1))
                        dve.wait_ge(wj_full, job_use(t, name, k) + 1)
                        d = xa[:, 2 * k:2 * k + 2, :].rearrange("p t n -> p (t n)")
                        nc.vector.tensor_tensor(d, wj_b[:, 0, :], d, ALU.add).then_inc(wj_free, 1)
                    elif name == "stats":
                        k = arg[0]
                        n = t.JA if k else t.J
                        if k:
                            dve.wait_ge(wj_free, job_use(t, "y", 1) + 1)
                        elif t.job == JOB_A:
                            dve.wait_ge(x_in, 16 * (t.J + 1))
                        else:
                            dve.wait_ge(wj_free, job_use(t, "wo", 1) + 1)
                        for tk in range(GT):
                            last = nc.vector.bn_stats(bst[:, tk, :], xa[:, tk, :])
                        last.then_inc(stat1[k], 1)
                        dve.wait_ge(stat1[k], n + 1)
                        stand_dve(2)
                        for tk in range(GT):
                            last = nc.vector.bn_aggr(mv[:, tk, :], bst[:, tk, :])
                        last.then_inc(stat2[k], 1)
                    elif name == "norm":
                        k = arg[0]
                        n = t.JA if k else t.J
                        dve.wait_ge(rstd[k], n + 1)
                        for tk in range(GT):
                            last = nc.vector.tensor_scalar(xn[:, tk, :], xa[:, tk, :], mv[:, tk, 0:1], rs[:, tk:tk + 1],
                                                           ALU.subtract, ALU.mult)
                        last.then_inc(normed[k], 1)
                    elif name == "route":
                        k = arg[0]
                        n = RT * t.J
                        if k == 0:
                            dve.wait_ge(wj_free, job_use(t, "low", 1) + 1)
                            stand_dve(3)
                            for tk in range(GT):
                                last = nc.vector.max(m8[:, tk, :], hl[:, tk, ER:HLW])
                            last.then_inc(rt, 1)
                        elif k == 1:
                            dve.wait_ge(rt, n + 1)
                            stand_dve(4)
                            for tk in range(GT):
                                last = nc.vector.max_index(ix[:, tk, :], m8[:, tk, :], hl[:, tk, ER:HLW])
                            last.then_inc(rt, 1)
                        elif k == 2:
                            nc.vector.tensor_tensor(ls[:, :, :], hl[:, :, ER:HLW],
                                                    m8[:, :, 0:1].to_broadcast([P, GT, E]), ALU.subtract).then_inc(rt, 1)
                        elif k == 3:
                            dve.wait_ge(rt, n + 2)
                            nc.vector.tensor_copy(ixf[:, :, :], ix[:, :, 0:2]).then_inc(rt, 1)
                        elif k == 4:
                            dve.wait_ge(rt, n + 4)
                            io = iota[:, :].unsqueeze(1).to_broadcast([P, GT, E])
                            nc.vector.tensor_tensor(k1m[:, :, :], io, ixf[:, :, 0:1].to_broadcast([P, GT, E]), ALU.is_equal)
                            nc.vector.tensor_tensor(k2m[:, :, :], io, ixf[:, :, 1:2].to_broadcast([P, GT, E]),
                                                    ALU.is_equal).then_inc(rt, 1)
                        elif k == 5:
                            dve.wait_ge(rt, n + 5)
                            dve.wait_ge(exped, t.J + 1)
                            nc.vector.tensor_tensor(msk[:, :, :], k1m[:, :, :], k2m[:, :, :], ALU.add)
                            nc.vector.tensor_reduce(se[:, :], ex[:, :, :], AX_X, ALU.add).then_inc(rt, 1)
                        elif k == 6:
                            dve.wait_ge(rt, n + 6)
                            nc.vector.tensor_tensor(em[:, :, :], ex[:, :, :], msk[:, :, :], ALU.mult).then_inc(rt, 1)
                        elif k == 7:
                            dve.wait_ge(rt, n + 7)
                            nc.vector.tensor_reduce(sm[:, :], em[:, :, :], AX_X, ALU.add).then_inc(rt, 1)
                        elif k == 8:
                            dve.wait_ge(rt, n + 8)
                            nc.vector.scalar_tensor_tensor(out=den[:, :], in0=se[:, :], scalar=GATE_EPS, in1=sm[:, :],
                                                           op0=ALU.mult, op1=ALU.add).then_inc(rt, 1)
                    elif name == "gated":
                        dve.wait_ge(rt, RT * t.J + 9)
                        nc.vector.reciprocal(rc[:, :], den[:, :]).then_inc(rcd, 1)
                        dve.wait_ge(rcd, t.J + 1)
                        nc.vector.tensor_tensor(gate[:, :, :], em[:, :, :],
                                                rc[:, :].unsqueeze(2).to_broadcast([P, GT, E]), ALU.mult).then_inc(gates, 1)
                    elif name == "y":
                        k = arg[0]
                        if k == 0:
                            dve.wait_ge(biased, t.J + 1)
                        dve.wait_ge(wj_full, job_use(t, name, k) + 1)
                        d = xa[:, 2 * k:2 * k + 2, :].rearrange("p t n -> p (t n)")
                        nc.vector.scalar_tensor_tensor(out=d, in0=wj_b[:, 0, :], scalar=0.5, in1=d, op0=ALU.mult,
                                                       op1=ALU.add).then_inc(wj_free, 1)
                    elif name == "ss":
                        dve.wait_ge(wj_full, job_use(t, name, 0) + 1)
                        nc.vector.tensor_scalar(ssv[:, :], wj_b[:, 0, 0:GT], 1.0 / KR, RMS_EPS, ALU.mult,
                                                ALU.add).then_inc(wj_free, 1)

            walk(dve, turn)

        @block.gpsimd
        def _(pool):
            nc.gpsimd.memset(ident[:, :], 0.0).then_inc(const, 1)
            nc.gpsimd.memset(tri[:, :], 0.0).then_inc(const, 1)
            nc.gpsimd.memset(powers[:, :], -0.5).then_inc(const, 1)
            nc.gpsimd.iota(iota[:, :], pattern=[[1, E]], base=0, channel_multiplier=0,
                           allow_small_or_imprecise_dtypes=True).then_inc(const, 1)
            for i in range(NQ):
                last = nc.gpsimd.memset(v_s[i][:, :, :, :], 1.0)
            last.then_inc(const, 1)
            pool.wait_ge(const, 8)
            nc.gpsimd.affine_select(out=ident[:, :], in_=ident[:, :], compare_op=ALU.not_equal, fill=1.0, base=0,
                                    pattern=[[-1, P]], channel_multiplier=1).then_inc(const, 1)
            nc.gpsimd.affine_select(out=tri[:, HALF - P:HALF], in_=tri[:, HALF - P:HALF], compare_op=ALU.is_ge,
                                    fill=-1.0e38, base=0, pattern=[[-1, P]], channel_multiplier=1).then_inc(const, 1)
            pool.wait_ge(const, 10)
            pool.wait_ge(w_in, 16 * N_W)
            pool.wait_ge(prep, 2)

            def turn(t):
                g, b, q = t.g, t.b, t.q
                for name, *arg in t.steps:
                    if name == "score" and arg[1] == HQ - 1 and ATT[arg[0]][4]:
                        s = arg[0]
                        pool.wait_ge(exp_done, UNITS * g + HQ * (s + 1))
                        stand_pool(5)
                        d = probs[:, s % 2, :, 0:P]
                        nc.gpsimd.affine_select(out=d, in_=d, compare_op=ALU.is_ge, fill=0.0, base=0,
                                                pattern=[[0, HQ], [1, P]], channel_multiplier=-1).then_inc(masked, 1)
                    elif name == "proj":
                        k = arg[0]
                        i = TB * (g + 1) + k
                        pool.wait_ge(wp_read, i + 1)
                        d = qk[:, i_par(k), :, :]
                        cs = cos_s[:, k, :].unsqueeze(1).to_broadcast([P, 2 * HQ, DR])
                        sn = sin_s[:, k, :].unsqueeze(1).to_broadcast([P, 2 * HQ, DR])
                        hd = DR // 2
                        nc.gpsimd.tensor_tensor(rot_c[:, :, :], d[:, :, DC:DQ], cs, ALU.mult)
                        nc.gpsimd.tensor_tensor(rot_s[:, :, 0:hd], d[:, :, DC + hd:DQ], sn[:, :, 0:hd], ALU.mult)
                        nc.gpsimd.tensor_tensor(rot_s[:, :, hd:DR], d[:, :, DC:DC + hd], sn[:, :, hd:DR],
                                                ALU.mult).then_inc(rot1, 1)
                        pool.wait_ge(rot1, i + 1)
                        nc.gpsimd.tensor_tensor(d[:, :, DC:DQ], rot_c[:, :, :], rot_s[:, :, :],
                                                ALU.add).then_inc(roped, 1)
                    elif name == "stats":
                        k = arg[0]
                        n = t.JA if k else t.J
                        pool.wait_ge(stat2[k], n + 1)
                        stand_pool(6)
                        nc.gpsimd.tensor_scalar(ve[:, :], mv[:, :, 1], LN_EPS, None, ALU.add).then_inc(rv[k], 1)
                        pool.wait_ge(rv[k], n + 1)
                        nc.gpsimd.tensor_tensor(rs[:, :], ve[:, :], powers[:, :], ALU.pow).then_inc(rstd[k], 1)
                    elif name == "norm" and arg[0] == 0:
                        pool.wait_ge(normed[0], t.J + 1)
                        nc.gpsimd.tensor_tensor(xa[:, :, :], xa[:, :, :],
                                                hb_s[:, :].unsqueeze(1).to_broadcast([P, GT, D]),
                                                ALU.add).then_inc(biased, 1)
                    elif name == "gated":
                        pool.wait_ge(gates, t.J + 1)
                        nc.gpsimd.tensor_tensor(gh.rearrange("p t (e r) -> p t e r", r=R),
                                                hl[:, :, 0:ER].rearrange("p t (e r) -> p t e r", r=R),
                                                gate[:, :, :].unsqueeze(3).to_broadcast([P, GT, E, R]),
                                                ALU.mult).then_inc(gated, 1)
                    elif name == "ss":
                        pool.wait_ge(wj_free, job_use(t, name, 0) + 1)
                        nc.gpsimd.tensor_tensor(stg[:, :, 3 * P], ssv[:, :], powers[:, :], ALU.pow).then_inc(r_done, 1)

            walk(pool, turn)


def kernel(L0_attn_x, L0_attn_W_kv, L0_attn_g_kv, L0_attn_W_kdec, L0_attn_W_vdec, L0_attn_W_q, L0_attn_W_qdec,
           L0_attn_W_krope, L0_attn_W_qrope, L0_attn_W_o, L0_ffn_W, L0_ffn_b, L0_ffn_R, L0_ffn_A, L0_ffn_B):
    import numpy as np
    import concourse.bacc as bacc
    from concourse.bass_utils import run_bass_kernel_spmd

    a = np.asarray
    inv_freq = 1.0 / 10000.0 ** (np.arange(0, DR, 2, dtype=np.float32) / DR)
    freqs = np.outer(np.arange(T, dtype=np.float32), inv_freq)
    emb = np.concatenate([freqs, freqs], -1)
    cos, sin = np.cos(emb), np.sin(emb)
    sin[:, :DR // 2] *= -1
    per_quad = lambda w, n: a(w).reshape(-1, NQ, HQ, n)
    arrays = {
        "x": a(L0_attn_x).reshape(B * T, D),
        "w1": np.concatenate([a(L0_ffn_W).T, a(L0_ffn_A).reshape(ER, D).T, a(L0_ffn_R).T], 1),
        "bt": a(L0_ffn_B).transpose(0, 2, 1).reshape(ER, D),
        "bias": a(L0_ffn_b),
        "wkvq": np.concatenate([a(L0_attn_W_kv), a(L0_attn_W_q)], 1),
        "wkr": a(L0_attn_W_krope).reshape(D, NQ, HQ * DR),
        "wkv": np.concatenate([a(L0_attn_W_kdec).reshape(KR, NQ, HQ * DC),
                               a(L0_attn_W_vdec).reshape(KR, NQ, HQ * DV)], 2),
        "g_kv": a(L0_attn_g_kv).reshape(KR, 1),
        "wq": np.concatenate([per_quad(L0_attn_W_qdec, DC), per_quad(L0_attn_W_qrope, DR)],
                             3).reshape(QR, NQ, HQ * DQ),
        "wo": a(L0_attn_W_o),
        "cos": cos.astype(np.float32).reshape(TB, P, DR).transpose(1, 0, 2),
        "sin": sin.astype(np.float32).reshape(TB, P, DR).transpose(1, 0, 2),
    }
    arrays = {"in_" + k: np.ascontiguousarray(v) for k, v in arrays.items()}
    nc = bacc.Bacc("TRN2", target_bir_lowering=False, num_devices=1, dynamic_dma_scratch_size=1024)
    args = [nc.dram_tensor(k, v.shape, F32, kind="ExternalInput").ap() for k, v in arrays.items()]
    out = nc.dram_tensor("out_y", (B * T, D), F32, kind="ExternalOutput").ap()
    nc.disable_value_cache = True
    build(nc, *args, out)
    r = run_bass_kernel_spmd(nc, [arrays], core_ids=[0])
    return r.results[0]["out_y"].reshape(B, T, D)
```

```python
from contextlib import ExitStack

import concourse.bass as bass
from concourse import mybir

F32 = mybir.dt.float32
F32R = mybir.dt.float32r
BF16 = mybir.dt.bfloat16
U32 = mybir.dt.uint32
ALU = mybir.AluOpType
ACT = mybir.ActivationFunctionType
AX_X = mybir.AxisListType.X

P = 128
B, T, D = 8, 1024, 256
H, DC, DR, DV = 16, 16, 32, 16
DQ = DC + DR
QR, KR = 128, 64
E, R = 8, 16
ER = E * R
KD = D // P
TB = T // P
HQ = 4
NQ = H // HQ
GT = 4
HALF = 512
WIDE = 256

PQ, PKR, PKC, PV_ = 0, HQ * DQ, HQ * DQ + HQ * DR, HQ * DQ + HQ * DR + HQ * DC
HLW = ER + E
STGW = 3 * P + 1
LN_EPS, RMS_EPS, GATE_EPS = 1e-5, 1e-6, 1e-6
NEG = -3.0e38
SCALE = float(DQ) ** -0.5

ATT = []
for h2 in range(T // HALF):
    for j in range((h2 + 1) * HALF // P):
        q0 = max(P * j, HALF * h2)
        ATT.append((h2, j, q0, HALF * (h2 + 1) - q0, q0 == P * j))
NS = len(ATT)
UNITS = NS * HQ
DIAG = [s for s in range(NS) if ATT[s][4]]
HALF_END = [max(s for s in range(NS) if ATT[s][0] == h2) for h2 in range(2)]

MXC = []
for i in range(TB):
    for a in range(HQ):
        for c in range(2):
            k0, k1 = HALF * c, min(HALF * (c + 1), P * (i + 1))
            if k1 > k0:
                MXC.append((a, i, c, k0, k1 - k0, k1 == P * (i + 1)))
NM = len(MXC)

ODD = 64
SHIFT = ODD + DQ
HT = TB // 2

JOB_A, JOB_C = "before attention", "after attention"
RT = 9


def mx_steps(i):
    return [m for m in range(NM) if MXC[m][1] == i]


LENGTH = 64
PROBS = 3

DVE_COST = {"low_half": 0.65, "mx_fold": 0.2, "o_read": 0.65, "o_rcp": 0.3, "o_mul": 0.4, "o_turn": 0.7, "stats": 0.7,
            "aggr": 0.5, "norm": 0.7, "wo": 0.7, "route": 0.25, "gated": 0.4, "y": 0.7, "ss": 0.2}

O_PARTS = ("o_read", "o_rcp", "o_mul", "o_turn")


PLAN = {
    "unit":        120,
    "o_gap":       2.2,
    "pv":          3.6,
    "wo":          11.0,
    "y_gap":       4.6,
    "wo_lag":      2.4,
    "job":         5.9,
    "norm":        4.5,
    "tr":          4.0,
    "tr_gap":      1.4,
    "y_end":       36.0,
    "y_lag":       2.0,
    "route":       14.0,
    "route_gap":   1.2,
    "gated":       1.7,
    "q_gap":       1.5,
    "mx":          0.35,
    "mx_from":     5.4,
    "mx_to":       62.3,
    "proj":        6.5,
    "turn":        1.3,
    "bias":        1.3,
    "bias_gap":    2.0,
    "hi_gap":      0.7,
    "tile_gap":    3.6,
    "half_gap":    1.3,
}


def plan(att, proj, job, tail, load_cur, first_proj=False, late=False):
    at = []

    def put(when, *step):
        at.append((when, len(at), step))

    cost = [ATT[n // HQ][3] + PLAN["unit"] for n in range(UNITS)]
    start = [LENGTH * sum(cost[:n]) / sum(cost) for n in range(UNITS + 1)]
    if tail:
        put(start[1], "pv_tail")
        for n, part in enumerate(O_PARTS):
            put(start[1] + (PLAN["o_gap"] * n if att else 0) + 0.1, part, 1)
    if job and not late:
        put(0 if att else start[1] + 0.3, "x_load")
    if att:
        for n in range(UNITS):
            put(start[n], "score", n // HQ, n % HQ)
        for s in range(NS - 1):
            put(start[HQ * (s + 1)] + PLAN["pv"], "pv", s)
        for n, part in enumerate(O_PARTS):
            put(start[HQ * (HALF_END[0] + 1)] + PLAN["pv"] + 0.1 + PLAN["o_gap"] * n, part, 0)
    if job:
        c = job == JOB_C
        ahead = start[HQ * (HALF_END[0] + 1)] + PLAN["pv"] + PLAN["o_gap"] * 3 + 0.2 if late else 0
        if late:
            put(ahead, "x_load")
        if c:
            put(ahead + PLAN["wo"], "wo", 0)
            put(ahead + PLAN["wo"] + PLAN["y_gap"], "wo", 1)
        u = ahead + PLAN["wo"] + PLAN["y_gap"] + PLAN["wo_lag"] if c else PLAN["job"]
        for k in range(1 if c else 2):
            v = u + (PLAN["y_end"] if k else 0)
            put(v - 1, "stats", k, 0)
            put(v, "stats", k, 1)
            put(v + 1, "aggr", k)
            put(v + PLAN["norm"], "norm", k, 0)
            put(v + PLAN["norm"] + 1, "norm", k, 1)
        for k in range(GT):
            put(u + PLAN["norm"] + PLAN["bias"] + PLAN["bias_gap"] * k, "bias", k)
        for k in range(2):
            put(u + PLAN["norm"] + PLAN["tr"] + PLAN["tr_gap"] * k, "tr", k)
            put(u + PLAN["norm"] + PLAN["tr"] + PLAN["tr_gap"] * (k + 2), "low", k)
            put(u + PLAN["y_end"] - PLAN["y_lag"] + PLAN["y_gap"] * (k - 1), "y", k)
        for k in range(RT):
            put(u + PLAN["route"] + PLAN["route_gap"] * k, "route", k)
        put(u + PLAN["route"] + PLAN["route_gap"] * RT, "gated")
        put(u + PLAN["y_end"] - PLAN["y_lag"] - PLAN["y_gap"] - PLAN["gated"], "gated_tr")
        put(u + PLAN["y_end"] - 1.5, "x_store")
        if not c:
            v = u + PLAN["y_end"] + PLAN["norm"] + PLAN["tr"]
            put(v, "tr2", 0)
            put(v + PLAN["q_gap"], "tr2", 1)
            put(v + PLAN["q_gap"] * 2, "qc")
            put(v + PLAN["q_gap"] * 3, "kv")
            put(v + PLAN["q_gap"] * 4, "ss")
            put(v + PLAN["q_gap"] * 4 + 2, "nx_store")
    if proj:
        items = [("low_half", 0, 0), ("low_half", 0, 1)]
        for i in range(TB):
            ms = mx_steps(i)
            half = len(ms) // 2
            items += [("mx", m) for m in ms[:half - 1]]
            items += [("low_half", i + 1, 0)] if i + 1 < TB else []
            items += [("mx", ms[half - 1])]
            items += [("low_half", i + 1, 1)] if i + 1 < TB else []
            items += [("mx", m) for m in ms[half:]]
            items += [("mx_fold", i // HT)] if i % HT == HT - 1 else []
        own = [DVE_COST[n] if n != "mx" else PLAN["mx"] + MXC[m][4] / 960 for n, m, *_ in items]
        others = sorted((w, DVE_COST[x[0]]) for w, _, x in at if x[0] in DVE_COST)

        def spread(scale):
            now, left, places = PLAN["mx_from"], list(others), []
            for (n, k, *e), d in zip(items, own):
                if n == "low_half":
                    now = max(now, PLAN["mx_from"] + PLAN["tile_gap"] * k + PLAN["half_gap"] * e[0])
                if first_proj and (n, k, *e) == ("low_half", HT, 0):
                    now = 2 * LENGTH
                while left and left[0][0] <= now:
                    now += left.pop(0)[1]
                places.append(now)
                now += d * scale
            return places, now

        scale = 1 if first_proj else next(c / 100 for c in range(300, 0, -1) if spread(c / 100)[1] <= PLAN["mx_to"])
        for (n, k, *e), now in zip(items, spread(scale)[0]):
            put(now, n, k, *e)
            if n == "low_half" and e[0] == 0:
                put(max(now - PLAN["proj"], 0), "proj", k)
                put(max(now - PLAN["turn"], 0), "turn", k)
                put(max(now - PLAN["turn"], 0) + 0.05, "hi", k, 0)
                put(max(now - PLAN["turn"], 0) + PLAN["hi_gap"], "hi", k, 1)
            elif n == "low_half":
                if k % HT == HT - 1:
                    put(now + 0.1, "k2", k // HT)
                if k == HT + 1:
                    put(now + 2, "mx_turn", 0)
                    put(now + 2.1, "shift", 0)
            elif n == "mx_fold" and k == 1:
                put(now + 1.5, "mx_turn", k)
                put(now + 1.6, "shift", k)
    if load_cur:
        put(60, "load_cur", 0)
        put(60, "load_cur", 1)
    if first_proj:
        put(0, "load_cur", 0)
        put(1.5 * LENGTH, "load_cur", 1)
    return [step for _, _, step in sorted(at)]


TP_USES = [(n, a[0]) for n, *a in plan(True, True, None, True, False) if n in ("turn", "mx_turn")]


def tp_use(t, name, k):
    return len(TP_USES) * (t.g + 1) + TP_USES.index((name, k))


def zero(n):
    return isinstance(n, int) and n == 0


def first(t, g):
    return isinstance(t.g, int) and t.g == g


def first_turn(t):
    return first(t, 0)


def first_proj(t):
    return first(t, -1)


class Turn:

    def __init__(self, b, q, att=True, proj=True, load_cur=False, job=None, tail=True, J=0, w=0, JA=0, JC=0, prev=None,
                 late=False):
        self.b, self.q, self.g = b, q, NQ * b + q
        self.att, self.proj, self.job, self.tail = att, proj, job, tail
        self.J, self.w, self.JA, self.JC, self.prev = J, w, JA, JC, prev
        self.late = late
        self.steps = plan(att, proj, job, tail, load_cur, isinstance(b, int) and self.g == -1, late)


def turns_before():
    none = dict(att=False, proj=False, tail=False)
    return [
        Turn(-1, 0, **none, job=JOB_A, J=0, w=0, JA=0),
        Turn(-1, 3, att=False, tail=False, job=JOB_A, J=1, w=12, JA=1, prev=JOB_A),
    ]


def turns_of(b, first=False, last=False):
    if first:
        J, w = 2, 24
    else:
        J, w = 4 * b, 48 + 42 * (b - 1)
    out = []
    for q in range(NQ):
        if last:
            out.append(Turn(b, q, proj=q < 3, job=JOB_C if q else None, J=J + q - 1, w=w + 9 * (q - 1),
                            JC=2 * (b - 1) + q - 1, prev=JOB_C, late=q == 3))
            continue
        a = q < 2
        job = None if not a and first else (JOB_A if a else JOB_C)
        prev = JOB_A if (first or 0 < q < 3) else JOB_C
        out.append(Turn(b, q, load_cur=q == 2, job=job, tail=not (first and q == 0), J=J + q,
                        w=w + (12 * q if a else 24 + 9 * (q - 2)), JA=2 * (b + 1) + q, JC=2 * (b - 1) + q - 2,
                        prev=prev))
    return out


def turns_after():
    none = dict(att=False, proj=False)
    w = 48 + 42 * (B - 2) + 27
    return [Turn(B, 0, **none, tail=True, job=JOB_C, J=4 * B - 1, w=w, JC=2 * B - 1, prev=JOB_C)]


def build(nc, x, w1, bt, bias, wkvq, wkr, wkv, g_kv, wq, wo, cos, sin, out):
    with ExitStack() as ctx:
        def sb(name, shape, dt=F32):
            return ctx.enter_context(nc.sbuf_tensor(name, shape, dt))

        def bank(name, n=1):
            return ctx.enter_context(nc.psum_tensor(name, [P, n, HALF], F32))

        def sem(name):
            return ctx.enter_context(nc.semaphore(name))

        x1_d = nc.dram_tensor("x1_scratch", (2 * B, P, GT, D), F32).ap()
        nx_d = nc.dram_tensor("nx_scratch", (2, P, GT, STGW), F32).ap()
        kv_d = nc.dram_tensor("kv_scratch", (2, KR, GT, P), F32).ap()
        sh_d = nc.dram_tensor("shift_scratch", (2, HQ * HT, P), F32).ap()
        ao_d = nc.dram_tensor("ao_scratch", (B, D, T), F32).ap()
        x_g = x.rearrange("(g t p) d -> g p t d", t=GT, p=P)
        out_g = out.rearrange("(g t p) d -> g p t d", t=GT, p=P)

        ident = sb("ident", [P, P])
        ones = sb("ones", [P, 2])
        tick = sb("tick", [P, 8 + len(DIAG)])
        tri = sb("tri", [P, HALF], BF16)
        iota = sb("iota", [P, E])
        powers = sb("powers", [P, GT])
        w1_s = sb("w1_s", [P, KD, D + HLW])
        bt_s = sb("bt_s", [P, D])
        hb_s = sb("hb_s", [P, D])
        wkvq_s = sb("wkvq_s", [P, KD, KR + QR])
        wkr_s = sb("wkr_s", [P, KD, NQ, HQ * DR])
        wkv_s = sb("wkv_s", [KR, NQ, 2 * HQ * DC])
        wq_s = sb("wq_s", [P, NQ, HQ * DQ])
        wo_s = sb("wo_s", [P, KD, D])
        cos_s = sb("cos_s", [P, TB, DR])
        sin_s = sb("sin_s", [P, TB, DR])
        g_s = sb("g_s", [KR, 1])

        st = [sb(f"st{i}", [P, 2, HQ, T], F32R) for i in range(2)]
        k2_st = [sb(f"k2_st{i}", [P, HQ, T], F32R) for i in range(2)]
        q_st = [s[:, 0] for s in st]
        k1_st = [s[:, 1] for s in st]
        v_s = [sb(f"v_s{i}", [P, TB, HQ, DV + 1]) for i in range(NQ)]
        probs = sb("probs", [P, PROBS, HQ, HALF])
        mx_s = sb("mx_s", [P, HQ * TB, 2])
        mxf = sb("mxf", [P, HQ * TB])
        shift = sb("shift", [HQ * HT, P], F32R)
        o_t = sb("o_t", [P, HALF // 32, 32])
        o_rc = sb("o_rc", [P, HALF // 32, 1])
        o_f = sb("o_f", [P, HALF])
        qk = sb("qk", [P, 2, 2 * HQ, ODD])
        rot_c = sb("rot_c", [P, 2, 2 * HQ, DR])
        rot_s = sb("rot_s", [P, 2, 2 * HQ, DR])
        cur = sb("cur", [P, TB, STGW])
        kvc = sb("kvc", [KR, TB, P])

        xa = sb("xa", [P, GT, D])
        xn = sb("xn", [P, GT, D])
        gh = xn[:, 0:2, :].rearrange("p a (t k) -> p (a t) k", k=ER)
        ght = xn[:, 2:4, :].rearrange("p a k -> p (a k)")
        xt = sb("xt", [P, GT, KD, P])
        hl = sb("hl", [P, GT, HLW])
        stg = sb("stg", [P, GT, STGW])
        kvs = sb("kvs", [KR, GT, P])
        ksq = sb("ksq", [KR, GT * P])
        aoc = sb("aoc", [P, KD, GT * P])
        bst = sb("bst", [P, GT, 6])
        mv = sb("mv", [P, GT, 2])
        ve = sb("ve", [P, GT])
        rs = sb("rs", [P, GT])
        ssv = sb("ssv", [P, GT])
        m8 = sb("m8", [P, GT, E])
        ix = sb("ix", [P, GT, E], U32)
        ixf = sb("ixf", [P, GT, 2])
        ls = sb("ls", [P, GT, E])
        ex = sb("ex", [P, GT, E])
        k1m = sb("k1m", [P, GT, E])
        k2m = sb("k2m", [P, GT, E])
        msk = sb("msk", [P, GT, E])
        em = sb("em", [P, GT, E])
        se = sb("se", [P, GT])
        sm = sb("sm", [P, GT])
        den = sb("den", [P, GT])
        rc = sb("rc", [P, GT])
        gate = sb("gate", [P, GT, E])

        st_b = bank("st_b", 2)
        mx_b = bank("mx_b", 2)
        o_b = bank("o_b")
        wp_b = bank("wp_b")
        tp_b = bank("tp_b")
        wj_b = bank("wj_b")

        w_in = sem("w_in")
        w2_in = sem("w2_in")
        blanked = sem("blanked")
        folded = sem("folded")
        const = sem("const")
        prep = sem("prep")
        x_in, ao_in = sem("x_in"), sem("ao_in")
        stored, nx_out, ao_out = sem("stored"), sem("nx_out"), sem("ao_out")
        cur_in = [sem("cur_in0"), sem("cur_in1")]
        k2_in, shift_in, shift_out = sem("k2_in"), sem("shift_in"), sem("shift_out")
        st_full, exp_done, masked = sem("st_full"), sem("exp_done"), sem("masked")
        pv_done, o_read, o_rcp, o_nrm, o_ready = (sem("pv_done"), sem("o_read"), sem("o_rcp"), sem("o_nrm"),
                                                  sem("o_ready"))
        mx_full, mx_done, mx_folded = sem("mx_full"), sem("mx_done"), sem("mx_folded")
        wp_full, wp_read, roped, rot1 = sem("wp_full"), sem("wp_read"), sem("roped"), sem("rot1")
        tp_full, hi_done, tp_free = sem("tp_full"), sem("hi_done"), sem("tp_free")
        wj_full, wj_free = sem("wj_full"), sem("wj_free")
        stat1 = [sem("stat1_0"), sem("stat1_1")]
        stat2 = [sem("stat2_0"), sem("stat2_1")]
        rv = [sem("rv_0"), sem("rv_1")]
        rstd = [sem("rstd_0"), sem("rstd_1")]
        normed = [sem("normed_0"), sem("normed_1")]
        biased = sem("biased")
        rt = sem("rt")
        exped = sem("exped")
        rcd, gates, gated = sem("rcd"), sem("gates"), sem("gated")
        ss_read, r_done = sem("ss_read"), sem("r_done")

        N_W, N_W2 = 3, 8
        block = ctx.enter_context(nc.Block())

        def walk(eng, turn):
            for t in turns_before() + turns_of(0, first=True):
                turn(t)
            with eng.Fori(1, B - 1) as b:
                for t in turns_of(b):
                    turn(t)
            for t in turns_of(B - 1, last=True) + turns_after():
                turn(t)

        def stand_dve(c):
            nc.vector.tensor_copy(tick[:, c:c + 1], ones[:, 0:1])

        def stand_pool(c):
            nc.gpsimd.tensor_tensor(tick[:, c:c + 1], powers[:, 0:1], powers[:, 1:2], ALU.add)

        def f32(tensor):
            return tensor[tuple(slice(None) for _ in tensor.shape)].bitcast(F32)

        def heads(tensor, e, k):
            return tensor.rearrange("p s (y e) t -> p s y e t", e=2)[:, :, :, e, P * k:P * k + P]

        def job_use(t, name, k):
            order = ["tr0", "tr1", "low0", "low1", "gated_tr0", "y0", "y1"]
            if t.job == JOB_A:
                order += ["tr20", "tr21", "qc0", "kv0", "ss0"]
            else:
                order = ["wo0", "wo1"] + order
            return t.w + order.index(f"{name}{k}")

        @block.sync
        def _(sp):
            sp.dma_start(w1_s[:, :, :], w1.rearrange("(k p) n -> p k n", p=P)).then_inc(w_in, 16)
            sp.dma_start(bt_s[:, :], bt).then_inc(w_in, 16)
            sp.dma_start(hb_s[:, :], bias.rearrange("(a n) -> a n", a=1).to_broadcast([P, D])).then_inc(w_in, 16)

            def load_attention():
                sp.dma_start(wkvq_s[:, :, :], wkvq.rearrange("(k p) n -> p k n", p=P)).then_inc(w2_in, 16)
                sp.dma_start(wkr_s[:, :, :, :], wkr.rearrange("(k p) q n -> p k q n", p=P)).then_inc(w2_in, 16)
                sp.dma_start(wkv_s[:, :, :], wkv).then_inc(w2_in, 16)
                sp.dma_start(g_s[:, :], g_kv).then_inc(w2_in, 16)
                sp.dma_start(wq_s[:, :, :], wq).then_inc(w2_in, 16)
                sp.dma_start(wo_s[:, :, :], wo.rearrange("(k p) n -> p k n", p=P)).then_inc(w2_in, 16)
                sp.dma_start(cos_s[:, :, :], cos).then_inc(w2_in, 16)
                sp.dma_start(sin_s[:, :, :], sin).then_inc(w2_in, 16)

            def turn(t):
                g, b, q = t.g, t.b, t.q
                u = q % 2
                for name, *arg in t.steps:
                    if name == "x_load":
                        if t.prev is not None:
                            sp.wait_ge(stored, 16 * t.J)
                        if t.prev == JOB_A:
                            sp.wait_ge(normed[1], t.JA if t.job == JOB_A else 2 * b + 4)
                        if t.job == JOB_A:
                            sp.dma_start(xa[:, :, :], x_g[t.JA]).then_inc(x_in, 16)
                            if zero(t.J):
                                load_attention()
                        else:
                            sp.dma_start(xa[:, :, :], x1_d[t.JC]).then_inc(x_in, 16)
                            bb = b if t.late else b - 1
                            half = t.JC % 2 if isinstance(t.JC, int) else q % 2
                            sp.wait_ge(ao_out, 128 * NQ * (bb + 1) - 64 * t.late)
                            sp.wait_ge(wj_full, t.w)
                            sp.dma_start(aoc[:, :, :], ao_d[bb].rearrange("(k p) t -> p k t", p=P)[
                                :, :, GT * P * half:GT * P * (half + 1)]).then_inc(ao_in, 16)
                    elif name == "x_store":
                        sp.wait_ge(wj_free, job_use(t, "y", 1) + 1)
                        if t.job == JOB_A:
                            sp.dma_start(x1_d[t.JA], xa[:, :, :]).then_inc(stored, 16)
                        else:
                            sp.dma_start(out_g[t.JC], xa[:, :, :]).then_inc(stored, 16)
                    elif name == "nx_store":
                        sp.wait_ge(r_done, t.JA + 1)
                        sp.wait_ge(wj_free, job_use(t, "kv", 0) + 1)
                        if not (isinstance(b, int) and b < 0):
                            sp.wait_ge(cur_in[q % 2], 32 * (b + 1))
                        sp.dma_start(nx_d[q % 2], stg[:, :, :]).then_inc(nx_out, 16)
                        sp.dma_start(kv_d[q % 2], kvs[:, :, :]).then_inc(nx_out, 16)
                    elif name == "load_cur":
                        h2 = arg[0]
                        n = 2 * (b + 1) + h2 + 1
                        sp.wait_ge(nx_out, 32 * n)
                        if not (isinstance(b, int) and b < 0):
                            sp.wait_ge(wp_full, TB * NQ * (b + 1))
                            sp.wait_ge(wp_read, TB * NQ * (b + 1))
                        cols = slice(HT * h2, HT * (h2 + 1))
                        sp.dma_start(cur[:, cols, :], nx_d[h2]).then_inc(cur_in[h2], 16)
                        sp.dma_start(kvc[:, cols, :], kv_d[h2]).then_inc(cur_in[h2], 16)
                    elif name == "k2":
                        h2, v = arg[0], (q + 1) % 2
                        sp.wait_ge(tp_free, tp_use(t, "turn", HT * h2 + HT - 1) + 1)
                        k1, k2, cols = f32(st[v])[:, 1], f32(k2_st[v]), slice(HALF * h2, HALF * (h2 + 1))
                        sp.dma_start(k2[0:DQ, :, cols], k1[ODD:SHIFT, :, cols]).then_inc(k2_in, 16)
                        sp.dma_start(k2[ODD:SHIFT, :, cols], k1[0:DQ, :, cols]).then_inc(k2_in, 16)
                    elif name == "shift":
                        h2, v = arg[0], (q + 1) % 2
                        n = 2 * (g + 1) + h2
                        sp.wait_ge(tp_free, tp_use(t, "mx_turn", h2) + 1)
                        sp.dma_start(sh_d[h2], f32(shift)).then_inc(shift_out, 16)
                        sp.wait_ge(shift_out, 16 * (n + 1))
                        sp.dma_start(f32(st[v])[SHIFT:SHIFT + 1, 0, :, HALF * h2:HALF * (h2 + 1)],
                                     sh_d[h2].rearrange("(a i) c -> a (i c)", a=HQ).unsqueeze(0)).then_inc(shift_in, 16)
                    elif name == "o_turn":
                        h2 = arg[0]
                        gg = g if h2 == 0 else g - 1
                        bb, qq = (b, q) if h2 == 0 else (b, q - 1) if q else (b - 1, NQ - 1)
                        sp.wait_ge(o_ready, 2 * gg + h2 + 1)
                        for a in range(HQ):
                            row = HQ * DV * qq + DV * a
                            sp.dma_start(ao_d[bb][row:row + DV, HALF * h2:HALF * (h2 + 1)],
                                         o_f[32 * a:32 * a + DV, :]).then_inc(ao_out, 16)

            walk(sp, turn)
            sp.wait_ge(stored, 16 * 4 * B)
            sp.wait_ge(nx_out, 64 * B)
            sp.wait_ge(ao_out, 128 * NQ * B)

        @block.tensor
        def _(pe):
            pe.wait_ge(w_in, 16 * N_W)
            pe.wait_ge(const, 10)

            def turn(t):
                g, b, q = t.g, t.b, t.q
                u = q % 2
                for name, *arg in t.steps:
                    g, q = t.g, t.q
                    if name == "score":
                        s, a = arg
                        h2, j, q0, n, _ = ATT[s]
                        i = UNITS * g + HQ * s + a
                        if j == 0 and a == 0:
                            pe.wait_ge(shift_in, 16 * (2 * g + h2 + 1))
                            pe.wait_ge(k2_in, 32 * (2 * g + h2 + 1))
                        if not (first_turn(t) and HQ * s + a < 2):
                            pe.wait_ge(exp_done, i - 1)
                        w = max(n, WIDE)
                        dst = st_b[:, a % 2, HALF - w:HALF]
                        q0 += n - w
                        nc.tensor.matmul(dst, k1_st[u][0:SHIFT + 1, a, P * j:P * j + P],
                                         q_st[u][0:SHIFT + 1, a, q0:q0 + w], start=True, stop=False)
                        nc.tensor.matmul(dst, k2_st[u][0:SHIFT, a, P * j:P * j + P],
                                         q_st[u][0:SHIFT, a, q0:q0 + w], start=False, stop=True).then_inc(st_full, 1)
                    elif name in ("pv", "pv_tail"):
                        s, g, q = (arg[0], t.g, t.q) if name == "pv" else (NS - 1, t.g - 1, (t.q - 1) % NQ)
                        h2, j, q0, n, diag = ATT[s]
                        if diag:
                            pe.wait_ge(masked, len(DIAG) * g + DIAG.index(s) + 1)
                        else:
                            pe.wait_ge(exp_done, UNITS * g + HQ * (s + 1))
                        if j == 0 and not (first_turn(t) and h2 == 0):
                            pe.wait_ge(o_read, 2 * g + h2)
                        for a in range(HQ):
                            last = nc.tensor.matmul(o_b[32 * a:32 * a + DV + 1, 0, q0 - HALF * h2:q0 - HALF * h2 + n],
                                                    v_s[q][:, j, a, :], probs[:, s % PROBS, a, 0:n],
                                                    start=(j == 0), stop=(s in HALF_END))
                        last.then_inc(pv_done, 1)
                    elif name == "mx":
                        m = arg[0]
                        a, i, c, k0, n, _ = MXC[m]
                        v = (q + 1) % 2
                        if m == 0 or MXC[m - 1][1] != i:
                            pe.wait_ge(tp_free, tp_use(t, "turn", i) + 1)
                        if not (first_proj(t) and m < 2):
                            pe.wait_ge(mx_done, NM * (g + 1) + m - 1)
                        w = max(n, min(WIDE, k0 + n))
                        nc.tensor.matmul(mx_b[:, m % 2, HALF - w:HALF], q_st[v][0:SHIFT, a, P * i:P * i + P],
                                         k1_st[v][0:SHIFT, a, k0 + n - w:k0 + n], start=True, stop=True).then_inc(mx_full, 1)
                    elif name == "mx_turn":
                        h2 = arg[0]
                        pe.wait_ge(mx_folded, 2 * (g + 1) + h2 + 1)
                        pe.wait_ge(tp_free, tp_use(t, name, h2))
                        nc.tensor.transpose(tp_b[0:HQ * HT, 0, 0:P], mxf[:, HQ * HT * h2:HQ * HT * (h2 + 1)],
                                            ident[:, :]).then_inc(tp_full, 1)
                    elif name == "proj":
                        k = arg[0]
                        i = TB * (g + 1) + k
                        r = (q + 1) % NQ
                        if first_proj(t) and k == 0:
                            pe.wait_ge(folded, 1)
                        if k % HT == 0:
                            pe.wait_ge(cur_in[k // HT], 32 * (b + 1 if q < 3 else b + 2))
                        if not (first_proj(t) and k == 0):
                            pe.wait_ge(wp_read, i)
                        nc.tensor.matmul(wp_b[:, 0, PQ:PKR], cur[:, k, 2 * P:3 * P], wq_s[:, r, :],
                                         start=True, stop=True)
                        for kk in range(KD):
                            nc.tensor.matmul(wp_b[:, 0, PKR:PKC], cur[:, k, kk * P:(kk + 1) * P], wkr_s[:, kk, r, :],
                                             start=(kk == 0), stop=(kk == KD - 1))
                        nc.tensor.matmul(wp_b[:, 0, PKC:PKC + 2 * HQ * DC], kvc[:, k, :], wkv_s[:, r, :],
                                         start=True, stop=True).then_inc(wp_full, 1)
                    elif name == "turn":
                        k = arg[0]
                        i = TB * (g + 1) + k
                        pe.wait_ge(roped, i + 1)
                        n = tp_use(t, name, k)
                        if not zero(n):
                            pe.wait_ge(tp_free, n)
                        flat = qk[:, k % 2, :, :].rearrange("p h c -> p (h c)")
                        for c in range(HALF // P):
                            last = nc.tensor.transpose(tp_b[:, 0, P * c:P * c + P], flat[:, P * c:P * c + P], ident[:, :])
                        last.then_inc(tp_full, 1)
                    elif name in ("wo", "tr", "low", "gated_tr", "y", "tr2", "qc", "kv", "ss"):
                        k = arg[0] if arg else 0
                        w = job_use(t, name, k)
                        if not (isinstance(w, int) and w == 0):
                            pe.wait_ge(wj_free, w)
                        wj = wj_b[:, 0, :]
                        if name == "wo":
                            if k == 0:
                                pe.wait_ge(ao_in, 16 * (t.JC + 1))
                            for tt in range(2):
                                for kk in range(KD):
                                    tk = 2 * k + tt
                                    last = nc.tensor.matmul(wj[:, D * tt:D * tt + D], aoc[:, kk, P * tk:P * tk + P],
                                                            wo_s[:, kk, :], start=(kk == 0), stop=(kk == KD - 1))
                        elif name in ("tr", "tr2"):
                            if k == 0:
                                n = t.J if name == "tr" else t.JA
                                pe.wait_ge(normed[name == "tr2"], n + 1)
                            for tt in range(2):
                                for kk in range(KD):
                                    c = KD * tt + kk
                                    last = nc.tensor.transpose(wj[:, P * c:P * c + P],
                                                               xn[:, 2 * k + tt, P * kk:P * kk + P], ident[:, :])
                        elif name == "low":
                            for tt in range(2):
                                for kk in range(KD):
                                    last = nc.tensor.matmul(wj[:, HLW * tt:HLW * tt + HLW], xt[:, 2 * k + tt, kk, :],
                                                            w1_s[:, kk, D:D + HLW], start=(kk == 0), stop=(kk == KD - 1))
                        elif name == "gated_tr":
                            pe.wait_ge(gated, t.J + 1)
                            for tk in range(GT):
                                last = nc.tensor.transpose(wj[:, P * tk:P * tk + P], gh[:, tk, :], ident[:, :])
                        elif name == "y":
                            for tt in range(2):
                                tk = 2 * k + tt
                                dst = wj[:, D * tt:D * tt + D]
                                for kk in range(KD):
                                    nc.tensor.matmul(dst, xt[:, tk, kk, :], w1_s[:, kk, 0:D], start=(kk == 0), stop=False)
                                last = nc.tensor.matmul(dst, ght[:, P * tk:P * tk + P], bt_s[:, :], start=False, stop=True)
                        elif name == "qc":
                            if zero(t.J):
                                pe.wait_ge(w2_in, 16 * N_W2)
                            for kk in range(KD):
                                last = nc.tensor.matmul(wj[:, :].rearrange("p (t c) -> p t c", c=P),
                                                        wkvq_s[:, kk, KR:KR + QR],
                                                        stg[:, :, kk * P:(kk + 1) * P], start=(kk == 0), stop=(kk == KD - 1))
                        elif name == "kv":
                            for kk in range(KD):
                                last = nc.tensor.matmul(wj[0:KR, :].rearrange("p (t c) -> p t c", c=P),
                                                        wkvq_s[:, kk, 0:KR],
                                                        stg[:, :, kk * P:(kk + 1) * P], start=(kk == 0), stop=(kk == KD - 1))
                        elif name == "ss":
                            for tk in range(GT):
                                last = nc.tensor.matmul(wj[:, tk:tk + 1], ksq[:, P * tk:P * tk + P], ones[0:KR, 0:1],
                                                        start=True, stop=True)
                        last.then_inc(wj_full, 1)

            walk(pe, turn)

        @block.scalar
        def _(act):
            act.wait_ge(const, 10)
            for stack, row, factor in ((st[0].rearrange("p s a t -> p (s a t)"), ODD - 32, 0.0),
                                       (k2_st[0].rearrange("p a t -> p (a t)"), ODD - 32, 0.0),
                                       (st[0].rearrange("p s a t -> p (s a t)")[:, HQ * T:], P - 32, 1.0)):
                rows = stack[row:row + 32]
                last = nc.scalar.activation(rows, ones[row:row + 32, 0:1].to_broadcast(rows.shape), ACT.Copy, scale=factor)
            last.then_inc(blanked, 1)

            def turn(t):
                g, b, q = t.g, t.b, t.q
                for name, *arg in t.steps:
                    if name == "score":
                        s, a = arg
                        n = ATT[s][3]
                        act.wait_ge(st_full, UNITS * g + HQ * s + a + 1)
                        if a == 0 and not (first_turn(t) and s < PROBS):
                            act.wait_ge(pv_done, NS * g + s - PROBS + 1)
                        nc.scalar.activation(probs[:, s % PROBS, a, 0:n], st_b[:, a % 2, HALF - n:HALF], ACT.Exp,
                                             scale=SCALE).then_inc(exp_done, 1)
                    elif name == "proj":
                        k = arg[0]
                        i = TB * (g + 1) + k
                        r = (q + 1) % NQ
                        act.wait_ge(wp_full, i + 1)
                        if not (first_proj(t) and k < 2):
                            act.wait_ge(tp_full, (tp_use(t, "turn", k - 2) if k > 1 else
                                                  tp_use(t, "turn", TB - 2 + k) - len(TP_USES)) + 1)
                        d = qk[:, k % 2, :, :]
                        src = wp_b[:, 0, :]
                        rms = cur[:, k, 3 * P:3 * P + 1]
                        nc.scalar.activation(d[:, 0:HQ, 0:DQ], src[:, PQ:PKR].rearrange("p (a c) -> p a c", c=DQ), ACT.Copy)
                        nc.scalar.activation(d[:, HQ:2 * HQ, DC:DQ],
                                             src[:, PKR:PKC].rearrange("p (a c) -> p a c", c=DR), ACT.Copy)
                        nc.scalar.activation(d[:, HQ:2 * HQ, 0:DC],
                                             src[:, PKC:PV_].rearrange("p (a c) -> p a c", c=DC), ACT.Copy, scale=rms)
                        nc.scalar.activation(v_s[r][:, k, :, 0:DV],
                                             src[:, PV_:PV_ + HQ * DV].rearrange("p (a c) -> p a c", c=DV), ACT.Copy,
                                             scale=rms).then_inc(wp_read, 1)
                    elif name == "hi":
                        k, e = arg
                        if e == 0:
                            act.wait_ge(tp_full, tp_use(t, "turn", k) + 1)
                        if e == 0 and k == 0 and isinstance(g, int) and g < 1:
                            act.wait_ge(blanked, g + 2)
                        rows = slice(ODD * e, ODD * e + DQ)
                        nc.scalar.activation(heads(st[(q + 1) % 2][rows], e, k),
                                             tp_b[rows, 0, :].rearrange("p (s y n) -> p s y n", s=2, n=P),
                                             ACT.Copy).then_inc(hi_done, 1)
                    elif name in ("tr", "low", "gated_tr", "tr2", "qc", "kv"):
                        k = arg[0] if arg else 0
                        act.wait_ge(wj_full, job_use(t, name, k) + 1)
                        wj = wj_b[:, 0, :]
                        if name == "tr":
                            dst, src = xt[:, 2 * k:2 * k + 2, :, :].rearrange("p t k n -> p (t k n)"), wj
                        elif name == "low":
                            dst = hl[:, 2 * k:2 * k + 2, :].rearrange("p t n -> p (t n)")
                            src = wj[:, 0:2 * HLW]
                        elif name == "gated_tr":
                            dst, src = ght, wj
                        elif name == "tr2":
                            if k == 0 and not (isinstance(t.JA, int) and t.JA == 0):
                                act.wait_ge(nx_out, 32 * t.JA)
                            dst = stg[:, 2 * k:2 * k + 2, 0:2 * P]
                            src = wj.rearrange("p (t n) -> p t n", n=2 * P)
                        elif name == "qc":
                            dst, src = stg[:, :, 2 * P:3 * P], wj.rearrange("p (t n) -> p t n", n=P)
                        elif name == "kv":
                            nc.scalar.activation(kvs[:, :, :].rearrange("p t n -> p (t n)"), wj[0:KR, :], ACT.Copy)
                            dst, src = ksq[:, :], wj[0:KR, :]
                        nc.scalar.activation(dst, src, ACT.Square if name == "kv" else ACT.Copy).then_inc(wj_free, 1)
                    elif name == "route" and arg[0] == 3:
                        act.wait_ge(rt, RT * t.J + 3)
                        nc.scalar.activation(ex[:, :, :], ls[:, :, :], ACT.Exp).then_inc(exped, 1)

            walk(act, turn)

        @block.vector
        def _(dve):
            nc.vector.memset(o_b[:, :, :], 0.0).then_inc(const, 1)
            nc.vector.memset(mx_s[:, :, :], NEG).then_inc(const, 1)
            nc.vector.memset(qk[:, :, :, :], 0.0)
            nc.vector.memset(ones[:, :], 1.0).then_inc(const, 1)
            dve.wait_ge(w_in, 16 * N_W)
            nc.vector.tensor_scalar(hb_s[:, :], hb_s[:, :], 0.5, None, ALU.mult).then_inc(prep, 1)
            dve.wait_ge(prep, 1)
            dve.wait_ge(const, 10)

            def turn(t):
                g, b, q = t.g, t.b, t.q
                for name, *arg in t.steps:
                    if name == "mx":
                        m = arg[0]
                        a, i, c, k0, n, diag = MXC[m]
                        dve.wait_ge(mx_full, NM * (g + 1) + m + 1)
                        if diag:
                            stand_dve(m % 2)
                        src = mx_b[:, m % 2, HALF - n:HALF]
                        dst = mx_s[:, HQ * HT * (i // HT) + HT * a + i % HT, c:c + 1]
                        if diag:
                            nc.vector.tensor_tensor_reduce(src, src, tri[:, HALF - n:HALF], 1.0, NEG, ALU.add,
                                                           ALU.max, dst).then_inc(mx_done, 1)
                        else:
                            nc.vector.tensor_reduce(dst, src, AX_X, ALU.max).then_inc(mx_done, 1)
                    elif name == "mx_fold":
                        h2 = arg[0]
                        n = 2 * (g + 1) + h2
                        dve.wait_ge(mx_done, NM * (g + 1) + max(mx_steps(HT * h2 + HT - 1)) + 1)
                        rows = slice(HQ * HT * h2, HQ * HT * (h2 + 1))
                        nc.vector.tensor_reduce(mxf[:, rows], mx_s[:, rows, :], AX_X, ALU.max).then_inc(mx_folded, 1)
                    elif name == "mx_turn":
                        h2 = arg[0]
                        n = 2 * (g + 1) + h2
                        dve.wait_ge(tp_full, tp_use(t, name, h2) + 1)
                        if not zero(n):
                            dve.wait_ge(shift_in, 16 * n)
                        nc.vector.tensor_scalar(shift[:, :], tp_b[0:HQ * HT, 0, 0:P], -1.0, None,
                                                ALU.mult).then_inc(tp_free, 1)
                    elif name in O_PARTS:
                        h2 = arg[0]
                        gg = g if h2 == 0 else g - 1
                        n = 2 * gg + h2
                        turned = o_t[:, :, :].rearrange("p a c -> p (a c)")
                        if name == "o_read":
                            if not zero(n):
                                dve.wait_ge(o_ready, n)
                            dve.wait_ge(pv_done, NS * gg + HALF_END[h2] + 1)
                            nc.vector.transpose(turned, o_b[:, 0, :]).then_inc(o_read, 1)
                        elif name == "o_rcp":
                            dve.wait_ge(o_read, n + 1)
                            nc.vector.reciprocal(o_rc[:, :, :], o_t[:, :, DV:DV + 1]).then_inc(o_rcp, 1)
                        elif name == "o_mul":
                            dve.wait_ge(o_rcp, n + 1)
                            nc.vector.tensor_tensor(o_t[:, :, 0:DV], o_t[:, :, 0:DV],
                                                    o_rc[:, :, :].to_broadcast([P, HALF // 32, DV]),
                                                    ALU.mult).then_inc(o_nrm, 1)
                        else:
                            dve.wait_ge(o_nrm, n + 1)
                            if not zero(n):
                                dve.wait_ge(ao_out, 64 * n)
                            nc.vector.transpose(o_f[:, :], turned).then_inc(o_ready, 1)
                    elif name == "low_half":
                        k, e = arg
                        i = TB * (g + 1) + k
                        dve.wait_ge(hi_done, 2 * i + e + 1)
                        rows, other = slice(ODD * e, ODD * e + DQ), slice(ODD * (1 - e), ODD * (1 - e) + DQ)
                        last = nc.vector.tensor_tensor(heads(st[(q + 1) % 2][other], e, k),
                                                       tp_b[rows, 0, :].rearrange("p (s y n) -> p s y n", s=2, n=P),
                                                       heads(f32(st[(q + 1) % 2])[rows], e, k), ALU.subtract)
                        if e:
                            last.then_inc(tp_free, 1)
                    elif name == "wo":
                        k = arg[0]
                        if k == 0:
                            dve.wait_ge(x_in, 16 * (t.J + 1))
                        dve.wait_ge(wj_full, job_use(t, name, k) + 1)
                        d = xa[:, 2 * k:2 * k + 2, :].rearrange("p t n -> p (t n)")
                        nc.vector.tensor_tensor(d, wj_b[:, 0, :], d, ALU.add).then_inc(wj_free, 1)
                    elif name == "stats":
                        k = arg[0]
                        n = t.JA if k else t.J
                        part = arg[1]
                        if part == 0 and k:
                            dve.wait_ge(wj_free, job_use(t, "y", 1) + 1)
                        elif part == 0 and t.job == JOB_A:
                            dve.wait_ge(x_in, 16 * (t.J + 1))
                        elif part == 0:
                            dve.wait_ge(wj_free, job_use(t, "wo", 1) + 1)
                        for tk in range(2 * part, 2 * part + 2):
                            last = nc.vector.bn_stats(bst[:, tk, :], xa[:, tk, :])
                        if part:
                            last.then_inc(stat1[k], 1)
                    elif name == "aggr":
                        k = arg[0]
                        n = t.JA if k else t.J
                        dve.wait_ge(stat1[k], n + 1)
                        stand_dve(2)
                        for tk in range(GT):
                            last = nc.vector.bn_aggr(mv[:, tk, :], bst[:, tk, :])
                        last.then_inc(stat2[k], 1)
                    elif name == "norm":
                        k, part = arg
                        n = t.JA if k else t.J
                        if part == 0:
                            dve.wait_ge(rstd[k], n + 1)
                        for tk in range(2 * part, 2 * part + 2):
                            last = nc.vector.tensor_scalar(xn[:, tk, :], xa[:, tk, :], mv[:, tk, 0:1], rs[:, tk:tk + 1],
                                                           ALU.subtract, ALU.mult)
                        if part:
                            last.then_inc(normed[k], 1)
                    elif name == "route":
                        k = arg[0]
                        n = RT * t.J
                        if k == 0:
                            dve.wait_ge(wj_free, job_use(t, "low", 1) + 1)
                            stand_dve(3)
                            for tk in range(GT):
                                last = nc.vector.max(m8[:, tk, :], hl[:, tk, ER:HLW])
                            last.then_inc(rt, 1)
                        elif k == 1:
                            dve.wait_ge(rt, n + 1)
                            stand_dve(4)
                            for tk in range(GT):
                                last = nc.vector.max_index(ix[:, tk, :], m8[:, tk, :], hl[:, tk, ER:HLW])
                            last.then_inc(rt, 1)
                        elif k == 2:
                            nc.vector.tensor_tensor(ls[:, :, :], hl[:, :, ER:HLW],
                                                    m8[:, :, 0:1].to_broadcast([P, GT, E]), ALU.subtract).then_inc(rt, 1)
                        elif k == 3:
                            dve.wait_ge(rt, n + 2)
                            nc.vector.tensor_copy(ixf[:, :, :], ix[:, :, 0:2]).then_inc(rt, 1)
                        elif k == 4:
                            dve.wait_ge(rt, n + 4)
                            io = iota[:, :].unsqueeze(1).to_broadcast([P, GT, E])
                            nc.vector.tensor_tensor(k1m[:, :, :], io, ixf[:, :, 0:1].to_broadcast([P, GT, E]), ALU.is_equal)
                            nc.vector.tensor_tensor(k2m[:, :, :], io, ixf[:, :, 1:2].to_broadcast([P, GT, E]),
                                                    ALU.is_equal).then_inc(rt, 1)
                        elif k == 5:
                            dve.wait_ge(rt, n + 5)
                            dve.wait_ge(exped, t.J + 1)
                            nc.vector.tensor_tensor(msk[:, :, :], k1m[:, :, :], k2m[:, :, :], ALU.add)
                            nc.vector.tensor_reduce(se[:, :], ex[:, :, :], AX_X, ALU.add).then_inc(rt, 1)
                        elif k == 6:
                            dve.wait_ge(rt, n + 6)
                            nc.vector.tensor_tensor(em[:, :, :], ex[:, :, :], msk[:, :, :], ALU.mult).then_inc(rt, 1)
                        elif k == 7:
                            dve.wait_ge(rt, n + 7)
                            nc.vector.tensor_reduce(sm[:, :], em[:, :, :], AX_X, ALU.add).then_inc(rt, 1)
                        elif k == 8:
                            dve.wait_ge(rt, n + 8)
                            nc.vector.scalar_tensor_tensor(out=den[:, :], in0=se[:, :], scalar=GATE_EPS, in1=sm[:, :],
                                                           op0=ALU.mult, op1=ALU.add).then_inc(rt, 1)
                    elif name == "gated":
                        dve.wait_ge(rt, RT * t.J + 9)
                        nc.vector.reciprocal(rc[:, :], den[:, :]).then_inc(rcd, 1)
                        dve.wait_ge(rcd, t.J + 1)
                        nc.vector.tensor_tensor(gate[:, :, :], em[:, :, :],
                                                rc[:, :].unsqueeze(2).to_broadcast([P, GT, E]), ALU.mult).then_inc(gates, 1)
                    elif name == "y":
                        k = arg[0]
                        if k == 0:
                            dve.wait_ge(biased, t.J + 1)
                        dve.wait_ge(wj_full, job_use(t, name, k) + 1)
                        d = xa[:, 2 * k:2 * k + 2, :].rearrange("p t n -> p (t n)")
                        nc.vector.scalar_tensor_tensor(out=d, in0=wj_b[:, 0, :], scalar=0.5, in1=d, op0=ALU.mult,
                                                       op1=ALU.add).then_inc(wj_free, 1)
                    elif name == "load_cur" and first_proj(t) and arg[0] == 0:
                        dve.wait_ge(w2_in, 16 * N_W2)
                        nc.vector.tensor_scalar(wkv_s[:, :, :], wkv_s[:, :, :], g_s[:, 0:1], None,
                                                ALU.mult).then_inc(folded, 1)
                    elif name == "load_cur" and first_proj(t) and arg[0] == 1:
                        nc.vector.memset(f32(st[1])[ODD - 32:ODD, :, :, :], 0.0)
                        nc.vector.memset(f32(k2_st[1])[ODD - 32:ODD, :, :], 0.0)
                        nc.vector.memset(f32(st[1])[P - 32:P, 1, :, :], 1.0).then_inc(blanked, 1)
                        dve.wait_ge(blanked, 2)
                    elif name == "ss":
                        dve.wait_ge(wj_full, job_use(t, name, 0) + 1)
                        nc.vector.tensor_scalar(ssv[:, :], wj_b[:, 0, 0:GT], 1.0 / KR, RMS_EPS, ALU.mult,
                                                ALU.add).then_inc(wj_free, 1)

            walk(dve, turn)

        @block.gpsimd
        def _(pool):
            nc.gpsimd.memset(ident[:, :], 0.0).then_inc(const, 1)
            nc.gpsimd.memset(tri[:, :], 0.0).then_inc(const, 1)
            nc.gpsimd.memset(powers[:, :], -0.5).then_inc(const, 1)
            nc.gpsimd.iota(iota[:, :], pattern=[[1, E]], base=0, channel_multiplier=0,
                           allow_small_or_imprecise_dtypes=True).then_inc(const, 1)
            for i in range(NQ):
                last = nc.gpsimd.memset(v_s[i][:, :, :, :], 1.0)
            last.then_inc(const, 1)
            pool.wait_ge(const, 8)
            nc.gpsimd.affine_select(out=ident[:, :], in_=ident[:, :], compare_op=ALU.not_equal, fill=1.0, base=0,
                                    pattern=[[-1, P]], channel_multiplier=1).then_inc(const, 1)
            nc.gpsimd.affine_select(out=tri[:, HALF - P:HALF], in_=tri[:, HALF - P:HALF], compare_op=ALU.is_ge,
                                    fill=-1.0e38, base=0, pattern=[[-1, P]], channel_multiplier=1).then_inc(const, 1)
            pool.wait_ge(const, 10)
            pool.wait_ge(prep, 1)

            def turn(t):
                g, b, q = t.g, t.b, t.q
                for name, *arg in t.steps:
                    if name == "score" and arg[1] == HQ - 1 and ATT[arg[0]][4]:
                        s = arg[0]
                        pool.wait_ge(exp_done, UNITS * g + HQ * (s + 1))
                        stand_pool(8 + DIAG.index(s))
                        d = probs[:, s % PROBS, :, 0:P]
                        nc.gpsimd.affine_select(out=d, in_=d, compare_op=ALU.is_ge, fill=0.0, base=0,
                                                pattern=[[0, HQ], [1, P]], channel_multiplier=-1).then_inc(masked, 1)
                    elif name == "proj":
                        k = arg[0]
                        i = TB * (g + 1) + k
                        if first_proj(t) and k == 0:
                            pool.wait_ge(w2_in, 16 * N_W2)
                        pool.wait_ge(wp_read, i + 1)
                        d = qk[:, k % 2, :, :]
                        cs = cos_s[:, k, :].unsqueeze(1).to_broadcast([P, 2 * HQ, DR])
                        sn = sin_s[:, k, :].unsqueeze(1).to_broadcast([P, 2 * HQ, DR])
                        hd, rot_cos, rot_sin = DR // 2, rot_c[:, k % 2], rot_s[:, k % 2]
                        nc.gpsimd.tensor_tensor(rot_cos, d[:, :, DC:DQ], cs, ALU.mult)
                        nc.gpsimd.tensor_tensor(rot_sin[:, :, 0:hd], d[:, :, DC + hd:DQ], sn[:, :, 0:hd], ALU.mult)
                        nc.gpsimd.tensor_tensor(rot_sin[:, :, hd:DR], d[:, :, DC:DC + hd], sn[:, :, hd:DR],
                                                ALU.mult).then_inc(rot1, 1)
                        pool.wait_ge(rot1, i + 1)
                        nc.gpsimd.tensor_tensor(d[:, :, DC:DQ], rot_cos, rot_sin,
                                                ALU.add).then_inc(roped, 1)
                    elif name == "aggr":
                        k = arg[0]
                        n = t.JA if k else t.J
                        pool.wait_ge(stat2[k], n + 1)
                        stand_pool(6)
                        nc.gpsimd.tensor_scalar(ve[:, :], mv[:, :, 1], LN_EPS, None, ALU.add).then_inc(rv[k], 1)
                        pool.wait_ge(rv[k], n + 1)
                        nc.gpsimd.tensor_tensor(rs[:, :], ve[:, :], powers[:, :], ALU.pow).then_inc(rstd[k], 1)
                    elif name == "bias":
                        k = arg[0]
                        if k == 0:
                            pool.wait_ge(normed[0], t.J + 1)
                        last = nc.gpsimd.tensor_tensor(xa[:, k, :], xa[:, k, :], hb_s[:, :], ALU.add)
                        if k == GT - 1:
                            last.then_inc(biased, 1)
                    elif name == "gated":
                        pool.wait_ge(gates, t.J + 1)
                        nc.gpsimd.tensor_tensor(gh.rearrange("p t (e r) -> p t e r", r=R),
                                                hl[:, :, 0:ER].rearrange("p t (e r) -> p t e r", r=R),
                                                gate[:, :, :].unsqueeze(3).to_broadcast([P, GT, E, R]),
                                                ALU.mult).then_inc(gated, 1)
                    elif name == "ss":
                        pool.wait_ge(wj_free, job_use(t, name, 0) + 1)
                        nc.gpsimd.tensor_tensor(stg[:, :, 3 * P], ssv[:, :], powers[:, :], ALU.pow).then_inc(r_done, 1)

            walk(pool, turn)


def kernel(L0_attn_x, L0_attn_W_kv, L0_attn_g_kv, L0_attn_W_kdec, L0_attn_W_vdec, L0_attn_W_q, L0_attn_W_qdec,
           L0_attn_W_krope, L0_attn_W_qrope, L0_attn_W_o, L0_ffn_W, L0_ffn_b, L0_ffn_R, L0_ffn_A, L0_ffn_B):
    import numpy as np
    import concourse.bacc as bacc
    from concourse.bass_utils import run_bass_kernel_spmd

    a = np.asarray
    inv_freq = 1.0 / 10000.0 ** (np.arange(0, DR, 2, dtype=np.float32) / DR)
    freqs = np.outer(np.arange(T, dtype=np.float32), inv_freq)
    emb = np.concatenate([freqs, freqs], -1)
    cos, sin = np.cos(emb), np.sin(emb)
    sin[:, :DR // 2] *= -1
    per_quad = lambda w, n: a(w).reshape(-1, NQ, HQ, n)
    arrays = {
        "x": a(L0_attn_x).reshape(B * T, D),
        "w1": np.concatenate([a(L0_ffn_W).T, a(L0_ffn_A).reshape(ER, D).T, a(L0_ffn_R).T], 1),
        "bt": a(L0_ffn_B).transpose(0, 2, 1).reshape(ER, D),
        "bias": a(L0_ffn_b),
        "wkvq": np.concatenate([a(L0_attn_W_kv), a(L0_attn_W_q)], 1),
        "wkr": a(L0_attn_W_krope).reshape(D, NQ, HQ * DR),
        "wkv": np.concatenate([a(L0_attn_W_kdec).reshape(KR, NQ, HQ * DC),
                               a(L0_attn_W_vdec).reshape(KR, NQ, HQ * DV)], 2),
        "g_kv": a(L0_attn_g_kv).reshape(KR, 1),
        "wq": np.concatenate([per_quad(L0_attn_W_qdec, DC), per_quad(L0_attn_W_qrope, DR)],
                             3).reshape(QR, NQ, HQ * DQ),
        "wo": a(L0_attn_W_o),
        "cos": cos.astype(np.float32).reshape(TB, P, DR).transpose(1, 0, 2),
        "sin": sin.astype(np.float32).reshape(TB, P, DR).transpose(1, 0, 2),
    }
    arrays = {"in_" + k: np.ascontiguousarray(v) for k, v in arrays.items()}
    nc = bacc.Bacc("TRN2", target_bir_lowering=False, num_devices=1, dynamic_dma_scratch_size=1024)
    args = [nc.dram_tensor(k, v.shape, F32, kind="ExternalInput").ap() for k, v in arrays.items()]
    out = nc.dram_tensor("out_y", (B * T, D), F32, kind="ExternalOutput").ap()
    nc.disable_value_cache = True
    build(nc, *args, out)
    r = run_bass_kernel_spmd(nc, [arrays], core_ids=[0])
    return r.results[0]["out_y"].reshape(B, T, D)
```
